# Optimizing a Trainium2 kernel written in Bass

```python
import numpy as np
import jax
import jax.numpy as jnp

def _softmax(x, axis=-1):
    return jax.nn.softmax(x, axis=axis)

def _gelu(x):
    return jax.nn.gelu(x, approximate=True)

def _silu(x):
    return jax.nn.silu(x)

def _sigmoid(x):
    return jax.nn.sigmoid(x)

def _layernorm(x, axis=-1, eps=1e-05):
    m = jnp.mean(x, axis=axis, keepdims=True)
    v = jnp.var(x, axis=axis, keepdims=True)
    return (x - m) / jnp.sqrt(v + eps)

def _scatter_add(tgt, idx, src, axis=0):
    return tgt.at[idx].add(src)

def _segment_sum(src, seg, n):
    return jax.ops.segment_sum(src, seg, n)
kernel_name = 'mk_early_fusion_d1_tok_img1024_r4_7d7561'

def setup_inputs(seed: int=0):
    np.random.seed(seed)
    _w = jnp.asarray

    def _rec_inputs():
        import jax
        import jax.numpy as jnp
        _rk = jax.random.key(seed)
        x = -0.000356955 + 1 * jax.random.normal(jax.random.fold_in(_rk, 1), (32, 3, 224, 224), jnp.float32)
        txt = -0.000394971 + 1.15376 * jax.random.normal(jax.random.fold_in(_rk, 2), (32, 128, 256), jnp.float32)
        return (x, txt)
    x, txt = _rec_inputs()

    def _L0_tok_setup():
        import jax, jax.numpy as jnp
        import numpy as np
        PATCH = 16
        H = W = 224
        C = 3
        NP_SIDE = H // PATCH
        NUM_PATCHES = NP_SIDE * NP_SIDE
        PATCH_DIM = C * PATCH * PATCH
        EMBED = 256
        key = jax.random.key(seed)
        k1, k2, k3, k4 = jax.random.split(key, 4)
        B = 128
        raw_pixels = jax.random.normal(k1, (B, C, H, W), dtype=jnp.float32)
        bound = 1.0 / np.sqrt(PATCH_DIM)
        W_embed = jax.random.uniform(k2, (PATCH_DIM, EMBED), minval=-bound, maxval=bound, dtype=jnp.float32)
        b_embed = jax.random.uniform(k3, (EMBED,), minval=-bound, maxval=bound, dtype=jnp.float32)
        pos_embed = jax.random.normal(k4, (1, NUM_PATCHES, EMBED), dtype=jnp.float32)
        return {'raw_pixels': raw_pixels, 'W_embed': W_embed, 'b_embed': b_embed, 'pos_embed': pos_embed}
    _L0_tok_all = _L0_tok_setup()
    _L0_tok_in = {k: v for k, v in _L0_tok_all.items() if k in ('W_embed', 'b_embed', 'pos_embed')}
    del _L0_tok_all

    def _L0_attn_setup():
        import jax, jax.numpy as jnp
        import numpy as np
        HIDDEN = 256
        HEADS = 8
        HEAD = HIDDEN // HEADS
        EPS = 1e-05

        def _gammas():
            lo = np.log(1.0 / 512.0)
            hi = np.log(1.0 / 32.0)
            lin = np.linspace(lo, hi, HEADS)
            return jnp.asarray(1.0 - np.exp(lin), dtype=jnp.float32)

        def _decay_mask(S, gammas):
            idx = jnp.arange(S)
            diff = idx[:, None] - idx[None, :]
            causal = diff >= 0
            safe = jnp.where(causal, diff, 0).astype(jnp.float32)
            D = jnp.where(causal[None], gammas[:, None, None] ** safe[None], 0.0)
            return D

        def _msr_forward(x, Wq, Wk, Wv, W1, W2, gn_w, gn_b):
            B, S, _ = x.shape
            xh = x.reshape(B, S, HEADS, HEAD)
            q = jnp.einsum('bshd,hde->bshe', xh, Wq)
            k = jnp.einsum('bshd,hde->bshe', xh, Wk)
            v = jnp.einsum('bshd,hde->bshe', xh, Wv)
            D = _decay_mask(S, _gammas())
            scores = jnp.einsum('bnhd,bmhd->bhnm', q, k) * D[None]
            ret = jnp.einsum('bhnm,bmhd->bnhd', scores, v)
            mu = jnp.mean(ret, axis=-1, keepdims=True)
            var = jnp.var(ret, axis=-1, keepdims=True)
            ret = (ret - mu) * jax.lax.rsqrt(var + EPS)
            ret = ret.reshape(B, S, HIDDEN) * gn_w + gn_b
            gated = x @ W1
            out = gated * jax.nn.sigmoid(gated) + ret
            return out @ W2
        key = jax.random.key(seed)
        ks = jax.random.split(key, 7)
        B, S = (2, 512)
        x = jax.random.normal(ks[0], (B, S, HIDDEN), dtype=jnp.float32)
        Wq = jax.random.normal(ks[1], (HEADS, HEAD, HEAD), dtype=jnp.float32) / HEAD
        Wk = jax.random.normal(ks[2], (HEADS, HEAD, HEAD), dtype=jnp.float32) / HEAD
        Wv = jax.random.normal(ks[3], (HEADS, HEAD, HEAD), dtype=jnp.float32) / HEAD
        W1 = jax.random.normal(ks[4], (HIDDEN, HIDDEN), dtype=jnp.float32) / HIDDEN
        W2 = jax.random.normal(ks[5], (HIDDEN, HIDDEN), dtype=jnp.float32) / HIDDEN
        gn_w = jnp.ones((HIDDEN,), dtype=jnp.float32)
        gn_b = jnp.zeros((HIDDEN,), dtype=jnp.float32)
        return {'x': x, 'Wq': Wq, 'Wk': Wk, 'Wv': Wv, 'W1': W1, 'W2': W2, 'gn_w': gn_w, 'gn_b': gn_b}
    _L0_attn_all = _L0_attn_setup()
    _L0_attn_in = {k: v for k, v in _L0_attn_all.items() if k in ('Wq', 'Wk', 'Wv', 'W1', 'W2', 'gn_w', 'gn_b')}
    del _L0_attn_all

    def _L0_ffn_setup():
        import jax, jax.numpy as jnp
        import numpy as np
        NUM_EXPERTS = 8
        EXPERT_CAPACITY = 2.0
        DIM = 256
        HIDDEN_DIM = 1024
        key = jax.random.key(seed)
        k_x, k_g, k_w1, k_w2 = jax.random.split(key, 4)
        n, t, d, f, e = (8, 256, DIM, HIDDEN_DIM, NUM_EXPERTS)
        x = jax.random.normal(k_x, (n, t, d), dtype=jnp.float32)
        gate_w = jax.random.normal(k_g, (e, d), dtype=jnp.float32) * 0.02
        w1 = jax.random.normal(k_w1, (e, d, f), dtype=jnp.float32) * 0.02
        w2 = jax.random.normal(k_w2, (e, f, d), dtype=jnp.float32) * 0.02
        return {'x': x, 'gate_w': gate_w, 'w1': w1, 'w2': w2}
    _L0_ffn_all = _L0_ffn_setup()
    _L0_ffn_in = {k: v for k, v in _L0_ffn_all.items() if k in ('gate_w', 'w1', 'w2')}
    del _L0_ffn_all
    return {'x': x, 'txt': txt, 'L0_tok_W_embed': _L0_tok_in['W_embed'], 'L0_tok_b_embed': _L0_tok_in['b_embed'], 'L0_tok_pos_embed': _L0_tok_in['pos_embed'], 'L0_attn_Wq': _L0_attn_in['Wq'], 'L0_attn_Wk': _L0_attn_in['Wk'], 'L0_attn_Wv': _L0_attn_in['Wv'], 'L0_attn_W1': _L0_attn_in['W1'], 'L0_attn_W2': _L0_attn_in['W2'], 'L0_attn_gn_w': _L0_attn_in['gn_w'], 'L0_attn_gn_b': _L0_attn_in['gn_b'], 'L0_ffn_gate_w': _L0_ffn_in['gate_w'], 'L0_ffn_w1': _L0_ffn_in['w1'], 'L0_ffn_w2': _L0_ffn_in['w2']}

def reference(x, txt, L0_tok_W_embed, L0_tok_b_embed, L0_tok_pos_embed, L0_attn_Wq, L0_attn_Wk, L0_attn_Wv, L0_attn_W1, L0_attn_W2, L0_attn_gn_w, L0_attn_gn_b, L0_ffn_gate_w, L0_ffn_w1, L0_ffn_w2):
    import jax
    import jax.numpy as jnp

    def _L0_tok_ref(raw_pixels, W_embed, b_embed, pos_embed):
        import jax, jax.numpy as jnp
        import numpy as np
        PATCH = 16
        H = W = 224
        C = 3
        NP_SIDE = H // PATCH
        NUM_PATCHES = NP_SIDE * NP_SIDE
        PATCH_DIM = C * PATCH * PATCH
        EMBED = 256
        B = raw_pixels.shape[0]
        patches = raw_pixels.reshape(B, C, NP_SIDE, PATCH, NP_SIDE, PATCH)
        patches = patches.transpose(0, 2, 4, 1, 3, 5).reshape(B, NUM_PATCHES, PATCH_DIM)
        x = jnp.einsum('bnd,de->bne', patches, W_embed) + b_embed
        return x + pos_embed

    def _L0_attn_ref(x, Wq, Wk, Wv, W1, W2, gn_w, gn_b):
        import jax, jax.numpy as jnp
        import numpy as np
        HIDDEN = 256
        HEADS = 8
        HEAD = HIDDEN // HEADS
        EPS = 1e-05

        def _gammas():
            lo = np.log(1.0 / 512.0)
            hi = np.log(1.0 / 32.0)
            lin = np.linspace(lo, hi, HEADS)
            return jnp.asarray(1.0 - np.exp(lin), dtype=jnp.float32)

        def _decay_mask(S, gammas):
            idx = jnp.arange(S)
            diff = idx[:, None] - idx[None, :]
            causal = diff >= 0
            safe = jnp.where(causal, diff, 0).astype(jnp.float32)
            D = jnp.where(causal[None], gammas[:, None, None] ** safe[None], 0.0)
            return D

        def _msr_forward(x, Wq, Wk, Wv, W1, W2, gn_w, gn_b):
            B, S, _ = x.shape
            xh = x.reshape(B, S, HEADS, HEAD)
            q = jnp.einsum('bshd,hde->bshe', xh, Wq)
            k = jnp.einsum('bshd,hde->bshe', xh, Wk)
            v = jnp.einsum('bshd,hde->bshe', xh, Wv)
            D = _decay_mask(S, _gammas())
            scores = jnp.einsum('bnhd,bmhd->bhnm', q, k) * D[None]
            ret = jnp.einsum('bhnm,bmhd->bnhd', scores, v)
            mu = jnp.mean(ret, axis=-1, keepdims=True)
            var = jnp.var(ret, axis=-1, keepdims=True)
            ret = (ret - mu) * jax.lax.rsqrt(var + EPS)
            ret = ret.reshape(B, S, HIDDEN) * gn_w + gn_b
            gated = x @ W1
            out = gated * jax.nn.sigmoid(gated) + ret
            return out @ W2
        return _msr_forward(x, Wq, Wk, Wv, W1, W2, gn_w, gn_b)

    def _L0_ffn_ref(x, gate_w, w1, w2):
        import jax, jax.numpy as jnp
        import numpy as np
        NUM_EXPERTS = 8
        EXPERT_CAPACITY = 2.0
        DIM = 256
        HIDDEN_DIM = 1024
        n, t, d = x.shape
        e = gate_w.shape[0]
        k = int(EXPERT_CAPACITY * t / e)
        scores = jnp.einsum('ntd,ed->nte', x, gate_w)
        probs = jax.nn.softmax(scores, axis=-1)
        g, m = jax.lax.top_k(probs.transpose(0, 2, 1), k)
        batch_idx = jnp.arange(n)[:, None, None]
        xin = x[batch_idx, m]
        h = jnp.einsum('nekd,edf->nekf', xin, w1)
        h = jax.nn.gelu(h, approximate=False)
        h = jnp.einsum('nekf,efd->nekd', h, w2)
        out_tok = g[..., None] * h
        out = jnp.zeros((n, t, d), dtype=x.dtype).at[batch_idx, m].add(out_tok)
        return out
    h = _L0_tok_ref(x, L0_tok_W_embed, L0_tok_b_embed, L0_tok_pos_embed)
    h = jnp.concatenate([h, txt], axis=1)
    h = h + _L0_attn_ref(_layernorm(h, axis=-1), L0_attn_Wq, L0_attn_Wk, L0_attn_Wv, L0_attn_W1, L0_attn_W2, L0_attn_gn_w, L0_attn_gn_b)
    h = h + _L0_ffn_ref(_layernorm(h, axis=-1), L0_ffn_gate_w, L0_ffn_w1, L0_ffn_w2)
    return h

_drawn_inputs = setup_inputs


def setup_inputs(seed=0):
    import zlib

    import numpy as np

    out = dict(_drawn_inputs(seed))
    spreads = {'L0_attn_gn_w': (1.0, 0.6), 'L0_attn_gn_b': (0.0, 0.8)}
    factors = {'L0_tok_b_embed': 3.805, 'L0_attn_W1': 31.393, 'L0_ffn_gate_w': 2.691}
    for name, (base, spread) in spreads.items():
        noise = np.random.default_rng([zlib.crc32(name.encode()), seed]).standard_normal(out[name].shape)
        drawn = base * np.exp(spread * noise) if base else spread * noise
        out[name] = jnp.asarray(drawn.astype(out[name].dtype))
    for name, factor in factors.items():
        out[name] = (out[name] * factor).astype(out[name].dtype)
    return out
```

```python
from contextlib import ExitStack

import concourse.bass as bass
from concourse import mybir

F32 = mybir.dt.float32
F16 = mybir.dt.float16
U32 = mybir.dt.uint32
I32 = mybir.dt.int32
ALU = mybir.AluOpType
ACT = mybir.ActivationFunctionType
AX = mybir.AxisListType
RADD_MAX = bass.bass_isa.ReduceOp.max

P = 128
B = 32
SIDE, PATCH = 14, 16
CIN = 3
WPIX = SIDE * PATCH
NPATCH = SIDE * SIDE
NTXT = 128
S = NPATCH + NTXT
D = 256
DH = D // P
HEADS, HD = 8, 32
HPH = P // HD
HP = NPATCH // 2
CH = ((0, HP), (HP, HP), (NPATCH, NTXT))
NE, FF = 8, 1024
FO = FF // P
CAP = 2 * S // NE
PAD = CAP + 1
G = 4
NG = B // G
SL = G * CAP
SC = ((0, 128), (128, 128), (256, SL - 256))
ROWS = NE * G
ROUNDS = (CAP + 7) // 8
NSENT = ROUNDS * 8 - CAP
RW = S + NSENT
EPS = 1e-5
JH = PATCH // 2
CI = CIN * PATCH
KE = 64 + CI
XS = 2048.0
WP = DH * FF + FO * D
NPH = 12

C_DQ = 0
C_DK = C_DQ + DH * S
C_KD = C_DK + DH * S
C_MASK = C_KD + 2 * HEADS
C_BD = C_MASK + P
C_ID = C_BD + P
C_TOK = C_ID + P
C_ROW = C_TOK + 3
C_ALL = C_ROW + 1


GAP = (0, 12, 2, 2, 4, 4, 4, 4, 16, 3, 14, 3)
GAP_ROUTE = 3
GAP_ROUND = 4
COST = {"gather": 4 * 0.972, "mm1": 6 * 0.324, "mm2": 12 * 0.256}


def expert_steps():
    steps = [("mm1", 0, 0), ("mm1", 0, 1)]
    for e in range(NE):
        steps += [("mm1", e, f) for f in range(2, FO)]
        if e + 1 < NE:
            steps += [("mm1", e + 1, 0), ("mm1", e + 1, 1)]
        steps += [("mm2", e, c, half) for c in range(3) for half in range(2)]
    return steps


def plan(attend, experts, prepare):
    front = []
    if attend:
        front = [(GAP[p], ("attn", s, p)) for s in range(G) for p in range(NPH)]
        front += [(GAP_ROUTE, ("route",)), (0, ("choose", -1))]
        front += [(GAP_ROUND, ("choose", r)) for r in range(ROUNDS)] + [(0, ("topk",))]
    back = []
    if experts:
        back = [("gather", s, half) for s in range(G) for half in range(2)] + expert_steps()
    if prepare:
        back = [(k, e) for e in range(NE) for k in ("prep_scale", "prep_split")]
    steps = []
    n = 0
    for gap, step in front:
        if prepare:
            n += step[0] == "attn" and step[2] in (1, 3, 8, 10)
            if n and back and step[0] == "attn" and step[2] in (1, 3, 8, 10):
                steps.append(back.pop(0))
        while experts and back and gap > 0:
            gap -= COST[back[0][0]]
            if gap < -2.5:
                break
            steps.append(back.pop(0))
        steps.append(step)
    return steps + back


def build(nc, x, txt, We, be, pos, Wq, Wk, Wv, W1, W2, gnw, gnb, gate, w1, w2, const, out):
    ctx = ExitStack()
    with ctx:
        def sb(name, shape, dt=F32):
            return ctx.enter_context(nc.sbuf_tensor(name, shape, dt))

        sems = []

        def sem(name):
            h = ctx.enter_context(nc.semaphore(name))
            sems.append(h)
            return h

        wscr = nc.dram_tensor("w_split", (NE, P, 2 * WP), F16, kind="Internal").ap()
        scr_idx = nc.dram_tensor("choice_index", (ROWS, PAD), F16, kind="Internal").ap()
        scr_slot = nc.dram_tensor("choice_slot", (ROWS * CAP, 2), F32, kind="Internal").ap()
        out_rows = out.rearrange("b s d -> (b s) d")

        cst = sb("cst", [P, C_ALL])
        dq = cst[:, C_DQ:C_DK].rearrange("p (h s) -> p h s", h=DH)
        dk = cst[:, C_DK:C_KD].rearrange("p (h s) -> p h s", h=DH)
        kd = cst[:, C_KD:C_MASK].rearrange("p (c h) -> p c h", c=2)
        mask = cst[:, C_MASK:C_BD]
        bd = cst[:, C_BD:C_ID]
        ident = cst[:, C_ID:C_TOK]
        tok = cst[:, C_TOK:C_ROW]
        rowbase = cst[0:ROWS, C_ROW:C_ALL]
        we = sb("we", [P, JH, D])
        posb = sb("posb", [P, 2, D])
        bebc = sb("bebc", [P, D])
        wqb = sb("wqb", [P, DH, P])
        wkvb = sb("wkvb", [P, DH, 2, P])
        wvraw = sb("wvraw", [P, DH, P])
        vsum = sb("vsum", [P, DH])
        w1g = sb("w1g", [P, DH, D])
        w2g = sb("w2g", [P, DH, D])
        gn = sb("gn", [P, 2, DH])
        gateT = sb("gateT", [P, DH, NE])
        nhalf = sb("nhalf", [P, 3 * HEADS])
        wsc = sb("wsc", [P, NE, 3])

        xt = sb("xt", [P, SIDE, WPIX])
        h = sb("h", [P, 2, 3, D])
        h2 = sb("h2", [P, 2, 3, D])
        st = sb("st", [P, 3, 6])
        mv = sb("mv", [P, 3, 2])
        ve = sb("ve", [P, 3])
        rs = sb("rs", [P, 3])
        xh = sb("xh", [P, 3, D])
        x2T = sb("x2T", [P, DH, 3 * P])
        xT = x2T[:, :, 0:S]
        qT = sb("qT", [P, DH, S])
        kT = sb("kT", [P, DH, S])
        kt = sb("kt", [P, 2, D])
        v = sb("v", [P, 3, D])
        s2 = sb("s2", [P, DH, S])
        s2b = s2
        sbd = sb("sbd", [P, DH, 2, P])
        sc = sb("sc", [P, 3, HEADS, P])
        sq = sb("sq", [P, 3, D])
        ss = sb("ss", [P, 3 * HEADS])
        ssb = sb("ssb", [P, 3 * HEADS])
        rg = sb("rg", [P, 3 * HEADS])
        rn = xh
        oT = sb("oT", [P, DH, S])
        th = oT
        st2 = sb("st2", [P, 3, 6])
        mv2 = sb("mv2", [P, 3, 2])
        ve2 = sb("ve2", [P, 3])
        rs2 = sb("rs2", [P, 3])
        rs2x = sb("rs2x", [P, 3])
        xs = sb("xs", [P, 3, D])
        lg = sb("lg", [P, 3, NE, G])
        lmax = sb("lmax", [P, 3, G])
        ldif = sb("ldif", [P, 3, NE, G])
        lexp = sb("lexp", [P, 3, NE, G])
        lsum = sb("lsum", [P, 3, G])
        lrec = sb("lrec", [P, 3, G])
        prob = sb("prob", [P, 3, NE, G])
        val = sb("val", [ROWS, 2, RW])
        top = sb("top", [ROWS, ROUNDS * 8])
        topi = sb("topi", [ROWS, ROUNDS * 8], U32)
        pack = sb("pack", [ROWS, CAP, 2])
        idx16 = sb("idx16", [ROWS, PAD], F16)

        xhl = sb("xhl", [P, 2, G, 3, D], F16)
        idxb = sb("idxb", [P, ROWS, PAD], F16)
        slot = sb("slot", [P, NE, 3, 2])

        sel = sb("sel", [P, 2, 3, NE * PAD], F16)
        slrow = sb("slrow", [P, NE, 3], U32)
        gs = sb("gs", [P, NE, 3])
        xin = sb("xin", [P, 2, DH, NE, SL], F16)
        wr = sb("wr", [P, 2, 2, WP], F16)
        h1f = sb("h1f", [P, 2, 2, SL])
        h1 = sb("h1", [P, 2, 2, FO, SL], F16)
        y = sb("y", [P, 2, 3, D])

        wst2 = xin[:, :, :, :, :].rearrange("p a b c d -> p (a b c d)").bitcast(F32)[:, 0:WP]
        am = sb("am", [P, 2])
        amr = sb("amr", [P, 2])
        amc = sb("amc", [P, 2])
        pw = sb("pw", [P, 2])
        pinv = sb("pinv", [P, 2])
        wscale = sb("wscale", [P, 2])

        pa = ctx.enter_context(nc.psum_tensor("pa", [P, 4, 512], F32))
        pf = ctx.enter_context(nc.psum_tensor("pf", [P, 4, 512], F32))

        d_x, d_h, d_w = sem("d_x"), [sem("d_txt0"), sem("d_txt1")], [sem("d_w0"), sem("d_w1")]
        d_out = [sem("d_out0"), sem("d_out1")]
        d_c1, d_c2, d_tail = sem("d_choice_out"), sem("d_slot_out"), sem("d_choice_in")
        d_scat, d_setup = sem("d_scatter"), sem("d_setup")
        names = ("embed", "xT", "qk", "vk", "gated_state", "scoresA", "scoresB", "ret", "retT", "w2", "x2T", "router")
        mm = [sem("mm_" + n) for n in names]
        (M_EMB, M_XT, M_QK, M_VK, M_GS, M_SA, M_SB, M_RET, M_RT, M_W2, M_X2T, M_RTR) = mm
        c_h, c_st, c_mv, c_ve, c_rs, c_xh = (sem("c_" + n) for n in ("h", "st", "mv", "ve", "rs", "xh"))
        c_xT, c_q, c_k, c_v, c_kt, c_th, c_s2, c_s2b, c_state = (
            sem("c_" + n) for n in ("xT", "q", "k", "v", "kt", "th", "s2", "s2b", "state"))
        c_scA, c_scB, c_sq, c_ss, c_ssb, c_rg, c_rn, c_oT, c_h2 = (
            sem("c_" + n) for n in ("scA", "scB", "sq", "ss", "ssb", "rg", "rn", "oT", "h2"))
        c_st2, c_mv2, c_ve2, c_rs2, c_rs2x, c_xs, c_hi, c_lo, c_x2T, c_lg = (
            sem("c_" + n) for n in ("st2", "mv2", "ve2", "rs2", "rs2x", "xs", "hi", "lo", "x2T", "lg"))
        c_soft, c_exp, c_prob, m_pT, c_val, c_top, c_pick = (
            sem("c_" + n) for n in ("soft", "exp", "prob", "pT", "val", "top", "pick"))
        c_sel, m_g, c_slot = sem("c_sel"), sem("mm_gather"), sem("c_slot")
        c_g = [sem("c_gather_act"), sem("c_gather_dve")]
        m_1, m_2, c_gelu, c_hh, c_hl, c_y = (sem(n) for n in ("mm_1", "mm_2", "c_gelu", "c_hh", "c_hl", "c_y"))
        p_am, p_amr, p_sc, p_hi, p_lo = (sem("p_" + n) for n in ("am", "amr", "sc", "hi", "lo"))
        p_out = [sem("p_out0"), sem("p_out1")]
        s_init, s_v, s_pool = sem("s_init"), sem("s_v"), sem("s_pool")

        def barrier():
            nc.sync.sem_clear(range(sems[0].num, sems[-1].num + 1))
            nc.all_engine_barrier(sem_only=True)

        def patches(t, j, c):
            rows = SIDE // 2
            return t[0:KE, rows * c:rows * (c + 1), :].rearrange("p a (b j) -> p a b j", j=PATCH)[:, :, :, j]

        def heads_bank(a, n, width):
            return a.rearrange("p b (h n) -> p b h n", h=2)[:, :, :, 0:n] if width == 256 else None

        with nc.Block(no_gpsimd_drain=True) as block:
            @block.sync
            def _(sp):
                sp.dma_start(cst[:, :], const).then_inc(d_setup, 16)
                sp.dma_start(posb[0:HP, :, :], pos[0].rearrange("(c p) d -> p c d", c=2)).then_inc(d_setup, 16)
                sp.dma_start(bebc[:, :], be.partition_broadcast(P)).then_inc(d_setup, 16)
                sp.dma_start(w1g[:, :, :], W1.rearrange("(h p) d -> p h d", h=DH)).then_inc(d_setup, 16)
                sp.dma_start(w2g[:, :, :], W2.rearrange("(h p) d -> p h d", h=DH)).then_inc(d_setup, 16)
                with nc.allow_non_contiguous_dma(reason="a few hundred words, once"):
                    sp.dma_start(gn[:, 0, :], gnw.rearrange("(h p) -> p h", h=DH)).then_inc(d_setup, 16)
                    sp.dma_start(gn[:, 1, :], gnb.rearrange("(h p) -> p h", h=DH)).then_inc(d_setup, 16)
                    for hf in range(DH):
                        sp.dma_start(gateT[:, hf, :], gate[:, hf * P:(hf + 1) * P].rearrange("e p -> p e"))\
                            .then_inc(d_setup, 16)
                sp.wait_ge(s_init, 4)
                rows = We.rearrange("(k j) e -> k j e", j=PATCH)
                for half in range(2):
                    sp.dma_start(we[64 * half:64 * half + CI, :, :], rows[:, JH * half:JH * (half + 1), :])\
                        .then_inc(d_setup, 16)
                for head in range(HEADS):
                    hf, r = head // HPH, head % HPH
                    a = slice(HD * r, HD * (r + 1))
                    sp.dma_start(wqb[a, hf, a], Wq[head]).then_inc(d_setup, 16)
                    sp.dma_start(wkvb[a, hf, 1, a], Wk[head]).then_inc(d_setup, 16)
                    sp.dma_start(wvraw[a, hf, a], Wv[head]).then_inc(d_setup, 16)
            n_setup = 16 * (9 + 2 + 3 * HEADS)

            @block.gpsimd
            def _(pool):
                pool.memset(xhl[:, :, :, :, :], 0.0).then_inc(s_pool, 1)
                pool.memset(xt[:, :, :], 0.0).then_inc(s_pool, 1)
                pool.memset(idx16[:, :], -5.0).then_inc(s_pool, 1)
                pool.memset(slot[:, :, :, :], 0.0).then_inc(s_pool, 1)
                pool.wait_ge(s_pool, 4)

            @block.vector
            def _(dve):
                dve.memset(we[:, :, :], 0.0).then_inc(s_init, 1)
                dve.memset(wqb[:, :, :], 0.0).then_inc(s_init, 1)
                dve.memset(wkvb[:, :, :, :], 0.0).then_inc(s_init, 1)
                dve.memset(wvraw[:, :, :], 0.0).then_inc(s_init, 1)
                dve.memset(h[:, :, :, :], 0.0)
                dve.memset(h2[:, :, :, :], 0.0)
                dve.memset(sq[:, :, :], 0.0)
                dve.memset(nhalf[:, :], -0.5)
                for k in range(NSENT):
                    dve.memset(val[:, 0, S + k:S + k + 1], 2.0 + k)
                dve.wait_ge(d_setup, n_setup)
                dve.tensor_tensor(posb[0:HP, :, :], posb[0:HP, :, :],
                                  bebc[0:HP, :].unsqueeze(1).broadcast_to([HP, 2, D]), ALU.add)
                dve.tensor_scalar(gn[:, :, :], gn[:, :, :], 2.0, None, ALU.mult)
                dve.tensor_scalar(w2g[:, :, :], w2g[:, :, :], 0.5, None, ALU.mult)
                dve.tensor_reduce(vsum[:, :], wvraw[:, :, :], AX.X, ALU.add).then_inc(s_v, 1)
                dve.wait_ge(s_v, 1)
                dve.tensor_scalar(vsum[:, :], vsum[:, :], -1.0 / HD, None, ALU.mult).then_inc(s_v, 1)
                dve.wait_ge(s_v, 2)
                for hf in range(DH):
                    dve.scalar_tensor_tensor(wkvb[:, hf, 0, :], wvraw[:, hf, :], vsum[:, hf:hf + 1], bd,
                                             ALU.add, ALU.mult)
        barrier()

        def body(g, attend, experts, prepare=False, more=True):
            steps = plan(attend, experts, prepare)

            def img(s):
                return g * G + s

            with nc.Block(no_gpsimd_drain=True) as block:
                @block.sync
                def _(sp):
                    def load_image(s):
                        if s:
                            sp.wait_ge(M_EMB, s)
                        for half in range(2):
                            for c in range(CIN):
                                a = slice(64 * half + PATCH * c, 64 * half + PATCH * (c + 1))
                                src = x[img(s), c].rearrange("(a i) w -> i a w", i=PATCH)
                                sp.dma_start(xt[a, :, 0:WPIX - JH * half], src[:, :, JH * half:WPIX])\
                                    .then_inc(d_x, 16)
                        if s >= 2:
                            sp.wait_ge(c_h2, s - 1)
                        sp.dma_start(h[:, s % 2, 2, :], txt[img(s)]).then_inc(d_h[s % 2], 16)

                    def load_weights(e, k):
                        sp.dma_start(wr[:, k, :, :].rearrange("p a b -> p (a b)"), wscr[e]).then_inc(d_w[k], 16)

                    def load_raw(e):
                        sp.dma_start(wst2[:, 0:DH * FF].rearrange("p (h f) -> p h f", h=DH),
                                     w1[e].rearrange("(h p) f -> p h f", h=DH)).then_inc(d_w[0], 16)
                        sp.dma_start(wst2[:, DH * FF:WP].rearrange("p (o d) -> p o d", o=FO),
                                     w2[e].rearrange("(o p) d -> p o d", o=FO)).then_inc(d_w[0], 16)

                    if attend:
                        load_image(0)
                    if prepare:
                        load_raw(0)
                    if experts:
                        load_weights(1, 1)
                    for step in steps:
                        if step[0] == "attn" and step[2] == 0 and step[1] + 1 < G:
                            load_image(step[1] + 1)
                        if step[0] == "attn" and step[2] == 9:
                            s = step[1]
                            sp.wait_ge(c_h2, s + 1)
                            rows = out[img(s)]
                            sp.dma_start(rows[0:NPATCH].rearrange("(c p) d -> p c d", c=2), h2[0:HP, s % 2, 0:2, :])\
                                .then_inc(d_out[s % 2], 16)
                            sp.dma_start(rows[NPATCH:S], h2[:, s % 2, 2, :]).then_inc(d_out[s % 2], 16)
                        if step[0] == "mm2" and step[2:] == (2, 1):
                            e = step[1]
                            if e + 2 < NE:
                                sp.wait_ge(m_2, 3 * e + 3)
                                load_weights(e + 2, e % 2)
                            elif e + 2 == NE and more:
                                sp.wait_ge(m_2, 3 * e + 3)
                                load_weights(0, 0)
                        if step[0] == "topk":
                            sp.wait_ge(c_pick, 2)
                            sp.dma_start(scr_idx, idx16[:, :]).then_inc(d_c1, 16)
                            sp.dma_start(scr_slot.rearrange("(r k) t -> r (k t)", r=ROWS),
                                         pack[:, :, :].rearrange("r k t -> r (k t)")).then_inc(d_c2, 16)
                            sp.wait_ge(d_c1, 16)
                            if experts:
                                sp.wait_ge(c_sel, G)
                            sp.dma_start(idxb[:, :, :].rearrange("p r k -> p (r k)"),
                                         scr_idx.rearrange("r k -> (r k)").partition_broadcast(P)).then_inc(d_tail, 16)
                            sp.wait_ge(d_c2, 16)
                            if experts:
                                sp.wait_ge(c_slot, 2)
                            per = scr_slot.rearrange("(e k) t -> e k t", e=NE)
                            with nc.allow_non_contiguous_dma(reason="two words per slot"):
                                for c, (k0, n) in enumerate(SC):
                                    sp.dma_start(slot[0:n, :, c, :], per[:, k0:k0 + n, :].rearrange("e k t -> k e t"))\
                                        .then_inc(d_tail, 16)
                        if step[0] == "prep_split":
                            e = step[1]
                            sp.wait_ge(p_hi, e + 1)
                            sp.wait_ge(p_lo, e + 1)
                            if e + 1 < NE:
                                load_raw(e + 1)
                            sp.dma_start(wscr[e], wr[:, e % 2, :, :].rearrange("p a b -> p (a b)"))\
                                .then_inc(p_out[e % 2], 16)
                    if prepare:
                        for k in range(2):
                            sp.wait_ge(p_out[k], 16 * (NE // 2))
                        sp.dma_start(wr[:, 0, :, :].rearrange("p a b -> p (a b)"), wscr[0]).then_inc(d_w[1], 16)
                        sp.wait_ge(d_w[1], 16)
                    if attend:
                        for k in range(2):
                            sp.wait_ge(d_out[k], 32 * (G // 2))
                        sp.wait_ge(d_tail, 16 * 4)
                    if experts and more:
                        sp.wait_ge(d_w[0], 16 * 4)

                @block.tensor
                def _(pe):
                    def embed(s):
                        pe.wait_ge(d_x, 96 * (s + 1))
                        if s:
                            pe.wait_ge(c_lg, s)
                        for c in range(2):
                            for j in range(JH):
                                last = pe.matmul(pa[0:HP, 0, D * c:D * (c + 1)], patches(xt, j, c), we[0:KE, j, :],
                                                 start=j == 0, stop=j == JH - 1)
                        last.then_inc(M_EMB, 1)

                    def turn(src, bank, pad):
                        for hf in range(DH):
                            for c, (t0, n) in enumerate(CH):
                                n, t0 = (P, P * c) if pad else (n, t0)
                                last = pe.transpose(pa[:, bank + hf, t0:t0 + n], src[0:n, c, P * hf:P * (hf + 1)],
                                                    ident[0:n, 0:n])
                        return last

                    def project_qk(s):
                        pe.wait_ge(c_xT, s + 1)
                        for k, w in enumerate((wqb, None)):
                            for hf in range(DH):
                                lhs = wqb[:, hf, :] if k == 0 else wkvb[:, hf, 1, :]
                                last = pe.matmul(pa[:, 2 * k + hf, 0:S], lhs, xT[:, hf, :], start=True, stop=True)
                        last.then_inc(M_QK, 1)

                    def project_vk(s):
                        pe.wait_ge(c_q, s + 1)
                        for c, (t0, n) in enumerate(CH):
                            if c == 2:
                                pe.wait_ge(c_k, s + 1)
                            w = 2 if c < 2 else 1
                            bank = pa[0:n, c, :].rearrange("p (w h e) -> p w h e", w=2, h=DH)
                            for hf in range(DH):
                                last = pe.matmul(bank[:, 0:w, hf, :], xT[:, hf, t0:t0 + n], wkvb[:, hf, 0:w, :],
                                                 start=hf == 0, stop=True, skip_group_check=True)
                        last.then_inc(M_VK, 1)

                    def gated_state(s):
                        for m in (1, 0):
                            if m == 0:
                                pe.wait_ge(c_v, s + 1)
                            for hf in range(DH):
                                pe.matmul(pa[:, 2 + m, 0:S], w1g[:, hf, P * m:P * (m + 1)], xT[:, hf, :],
                                          start=hf == 0, stop=hf == DH - 1)
                        pe.wait_ge(c_kt, s + 1)
                        for hf in range(DH):
                            for upto in range(2):
                                o = P * (2 * hf + upto)
                                for c in range(upto + 1):
                                    last = pe.matmul(pa[:, 0, o:o + P], kt[0:HP, c, P * hf:P * (hf + 1)],
                                                     v[0:HP, c, P * hf:P * (hf + 1)], start=c == 0, stop=c == upto)
                        last.then_inc(M_GS, 1)

                    def scores(c, place):
                        t0, n = CH[c]
                        for head in range(HEADS):
                            hf, r = head // HPH, head % HPH
                            a = slice(HD * r, HD * (r + 1))
                            o = 256 * place + P * hf
                            last = pe.matmul(pa[0:n, r, o:o + n], kT[a, hf, t0:t0 + n], qT[a, hf, t0:t0 + n],
                                             start=True, stop=True)
                        return last

                    def retain(s):
                        pe.wait_ge(c_scB, s + 1)
                        for c, (t0, n) in enumerate(CH):
                            o, bank = (D * c, 0) if c < 2 else (0, 1)
                            if c:
                                for hf in range(DH):
                                    pe.matmul(pa[0:n, bank, o + P * hf:o + P * (hf + 1)], qT[:, hf, t0:t0 + n],
                                              sbd[:, hf, c - 1, :], start=hf == 0, stop=False, skip_group_check=True)
                            for head in range(HEADS):
                                a = slice(HD * head, HD * (head + 1))
                                last = pe.matmul(pa[0:n, bank, o + HD * head:o + HD * (head + 1)],
                                                 sc[0:n, c, head, 0:n], v[0:n, c, a],
                                                 start=c == 0 and head == 0, stop=True, skip_group_check=True)
                        last.then_inc(M_RET, 1)

                    def mix(s):
                        pe.wait_ge(c_oT, s + 1)
                        for c, (t0, n) in enumerate(CH):
                            o, bank = (D * c, 0) if c < 2 else (0, 1)
                            for hf in range(DH):
                                last = pe.matmul(pa[0:n, bank, o:o + D], oT[:, hf, t0:t0 + n], w2g[:, hf, :],
                                                 start=hf == 0, stop=hf == DH - 1)
                        last.then_inc(M_W2, 1)

                    def attention(s, p):
                        if p == 0:
                            embed(s)
                        elif p == 1:
                            pe.wait_ge(c_xh, s + 1)
                            turn(xh, 1, False).then_inc(M_XT, 1)
                        elif p == 2:
                            project_qk(s)
                        elif p == 3:
                            project_vk(s)
                        elif p == 4:
                            gated_state(s)
                        elif p == 5:
                            pe.wait_ge(c_s2, s + 1)
                            pe.wait_ge(c_state, s + 1)
                            scores(0, 0)
                            scores(1, 1).then_inc(M_SA, 1)
                        elif p == 6:
                            pe.wait_ge(c_scA, s + 1)
                            scores(2, 0).then_inc(M_SB, 1)
                        elif p == 7:
                            retain(s)
                        elif p == 8:
                            pe.wait_ge(c_rn, s + 1)
                            turn(rn, 2, False).then_inc(M_RT, 1)
                        elif p == 9:
                            mix(s)
                        elif p == 10:
                            pe.wait_ge(c_xs, s + 1)
                            turn(xs, 2, True).then_inc(M_X2T, 1)
                        elif p == 11:
                            pe.wait_ge(c_x2T, s + 1)
                            for c in range(3):
                                for hf in range(DH):
                                    last = pe.matmul(pa[:, 0, NE * c:NE * (c + 1)], x2T[:, hf, P * c:P * (c + 1)],
                                                     gateT[:, hf, :], start=hf == 0, stop=hf == DH - 1)
                            last.then_inc(M_RTR, 1)

                    def gather(s, half):
                        pe.wait_ge(c_sel, s + 1)
                        for k in range(4 * half, 4 * half + 4):
                            n = 8 * s + k
                            part, hf, quad = k // 4, k // 2 % 2, k % 2
                            if n >= 4:
                                pe.wait_ge(c_g[n % 2], (n - 4) // 2 + 1)
                            for c in range(3):
                                rhs = sel[:, s % 2, c, :].rearrange("p (e k) -> p e k", k=PAD)[:, 4 * quad:4 * quad + 4, 0:CAP]
                                last = pe.matmul(pf[:, n % 4, 0:4 * CAP].rearrange("p (e k) -> p e k", k=CAP),
                                                 xhl[:, part, s, c, P * hf:P * (hf + 1)], rhs,
                                                 start=c == 0, stop=c == 2)
                            last.then_inc(m_g, 1)

                    def first(e, f):
                        m = FO * e + f
                        if m == 0:
                            pe.wait_ge(c_g[0], 4 * G)
                            pe.wait_ge(c_g[1], 4 * G)
                        if f == 0 and e:
                            pe.wait_ge(d_w[e % 2], 16 * ((e + 1) // 2))
                        if m >= 2:
                            pe.wait_ge(c_gelu, m - 1)
                        k = 0
                        for hf in range(DH):
                            for wp, xp in ((0, 0), (1, 0), (0, 1)):
                                o = FF * hf + P * f
                                last = pe.matmul(pf[:, m % 2, 0:SL], wr[:, e % 2, wp, o:o + P], xin[:, xp, hf, e, :],
                                                 start=k == 0, stop=k == 5)
                                k += 1
                        last.then_inc(m_1, 1)

                    def second(e, c, half):
                        k0, n = SC[c]
                        if c == 0 and half == 0:
                            pe.wait_ge(c_hl, 4 * e + 4)
                        if half == 0 and 3 * e + c >= 2:
                            pe.wait_ge(c_y, 3 * e + c - 1)
                        bank = 2 + (3 * e + c) % 2
                        k = 3 * FO // 2 * half
                        for f in range(FO // 2 * half, FO // 2 * (half + 1)):
                            for hp, wp in ((0, 0), (0, 1), (1, 0)):
                                o = DH * FF + D * f
                                last = pe.matmul(pf[0:n, bank, 0:D], h1[:, e % 2, hp, f, k0:k0 + n],
                                                 wr[:, e % 2, wp, o:o + D], start=k == 0, stop=k == 3 * FO - 1)
                                k += 1
                        if half:
                            last.then_inc(m_2, 1)

                    for step in steps:
                        if step[0] == "attn":
                            attention(*step[1:])
                        elif step[0] == "gather":
                            gather(*step[1:])
                        elif step[0] == "mm1":
                            first(*step[1:])
                        elif step[0] == "mm2":
                            second(*step[1:])
                        elif step[0] == "route":
                            pe.wait_ge(c_prob, 1)
                            for c, (t0, n) in enumerate(CH):
                                last = pe.transpose(pa[0:ROWS, 1, t0:t0 + n],
                                                    prob[0:n, c, :, :].rearrange("p e s -> p (e s)"), ident[0:n, 0:n])
                            last.then_inc(m_pT, 1)

                @block.scalar
                def _(act):
                    def attention(s, p):
                        if p == 1:
                            act.wait_ge(M_XT, s + 1)
                            act.copy(xT[:, :, :], pa[:, 1:3, 0:S]).then_inc(c_xT, 1)
                        elif p == 3:
                            act.wait_ge(M_VK, s + 1)
                            act.copy(v[0:HP, 0:2, :], pa[0:HP, 0:2, 0:D])
                            act.copy(v[:, 2, :], pa[:, 2, 0:D]).then_inc(c_v, 1)
                        elif p == 4:
                            act.wait_ge(M_GS, s + 1)
                            act.activation(th[:, :, :], pa[:, 2:4, 0:S], ACT.Tanh, scale=0.5).then_inc(c_th, 1)
                        elif p == 7:
                            act.wait_ge(M_RET, s + 1)
                            act.square(sq[0:HP, 0:2, :], pa[0:HP, 0, :].rearrange("p (c d) -> p c d", c=2))
                            act.square(sq[:, 2, :], pa[:, 1, 0:D]).then_inc(c_sq, 1)
                        elif p == 10:
                            act.wait_ge(c_xs, s + 1)
                            if experts:
                                act.wait_ge(m_g, 8 * (s + 1))
                            act.copy(xhl[:, 0, s, :, :], xs[:, :, :]).then_inc(c_hi, 1)
                            act.wait_ge(M_X2T, s + 1)
                            act.copy(x2T[:, :, :], pa[:, 2:4, 0:3 * P]).then_inc(c_x2T, 1)

                    def gathered(s, half):
                        for k in range(4 * half, 4 * half + 4, 2):
                            n = 8 * s + k
                            part, hf, quad = k // 4, k // 2 % 2, k % 2
                            act.wait_ge(m_g, n + 1)
                            act.copy(xin[:, part, hf, 4 * quad:4 * quad + 4, CAP * s:CAP * (s + 1)],
                                     pf[:, n % 4, 0:4 * CAP].rearrange("p (e k) -> p e k", k=CAP)).then_inc(c_g[0], 1)

                    for step in steps:
                        if step[0] == "attn":
                            attention(*step[1:])
                        elif step[0] == "gather":
                            gathered(*step[1:])
                        elif step[0] == "mm1":
                            e, f = step[1:]
                            m = FO * e + f
                            act.wait_ge(m_1, m + 1)
                            if m >= 4:
                                act.wait_ge(c_hl, m // 2 - 1)
                            act.activation(h1f[:, m // 2 % 2, m % 2, :], pf[:, m % 2, 0:SL], ACT.Gelu,
                                           scale=wsc[:, e, 0:1]).then_inc(c_gelu, 1)
                            if f % 2:
                                act.wait_ge(c_gelu, m + 1)
                                if f == 1 and e >= 2:
                                    act.wait_ge(m_2, 3 * (e - 1))
                                act.activation(h1[:, e % 2, 0, f - 1:f + 1, :], h1f[:, m // 2 % 2, :, :], ACT.Copy,
                                               scale=wsc[:, e, 1:2]).then_inc(c_hh, 1)
                        elif step[0] == "mm2" and step[3] == 1:
                            e, c = step[1:3]
                            n = SC[c][1]
                            act.wait_ge(m_2, 3 * e + c + 1)
                            if e == 0 and c == 0:
                                act.wait_ge(c_slot, 2)
                            if c == 0 and e >= 2:
                                act.wait_ge(d_scat, 48 * (e - 1))
                            act.activation(y[0:n, e % 2, c, :], pf[0:n, 2 + (3 * e + c) % 2, 0:D], ACT.Copy,
                                           scale=gs[0:n, e, c:c + 1]).then_inc(c_y, 1)
                        elif step[0] == "route":
                            act.wait_ge(c_soft, 2)
                            act.activation(lexp[:, :, :, :], ldif[:, :, :, :], ACT.Exp, scale=1.0 / XS)\
                                .then_inc(c_exp, 1)
                        elif step[0] == "prep_scale":
                            e = step[1]
                            act.wait_ge(p_sc, 4 * e + 4)
                            if e >= 2:
                                act.wait_ge(p_out[e % 2], 16 * (e // 2))
                            act.activation(wr[:, e % 2, 0, 0:DH * FF], wst2[:, 0:DH * FF], ACT.Copy,
                                           scale=wscale[:, 0:1])
                            act.activation(wr[:, e % 2, 0, DH * FF:WP], wst2[:, DH * FF:WP], ACT.Copy,
                                           scale=wscale[:, 1:2]).then_inc(p_hi, 1)

                @block.vector
                def _(dve):
                    def normalise(src, stats, means, n, done, scale, out_, c_stats, c_means, c_scale):
                        for c in range(3):
                            last = dve.bn_stats(stats[:, c, :], src[:, c, :])
                        last.then_inc(c_stats, 1)
                        dve.wait_ge(c_stats, n)
                        for c in range(3):
                            last = dve.bn_aggr(means[:, c, :], stats[:, c, :])
                        last.then_inc(c_means, 1)
                        dve.wait_ge(c_means, n)
                        dve.wait_ge(c_scale, n)
                        for c in range(3):
                            last = dve.tensor_scalar(out_[:, c, :], src[:, c, :], means[:, c, 0:1], scale[:, c:c + 1],
                                                     ALU.subtract, ALU.mult)
                        last.then_inc(done, 1)

                    def score_mask(s, c, place):
                        n = CH[c][1]
                        src = pa[0:n, :, 256 * place:256 * (place + 1)].rearrange("p r (h n) -> p r h n", h=2)[:, :, :, 0:n]
                        dst = sc[0:n, c, :, 0:n].rearrange("p (h r) n -> p r h n", h=2)
                        m = mask[0:n, 0:n].unsqueeze(1).unsqueeze(1).broadcast_to([n, HPH, 2, n])
                        return dve.tensor_tensor(dst, src, m, ALU.mult)

                    def attention(s, p):
                        if p == 0:
                            dve.wait_ge(M_EMB, s + 1)
                            dve.wait_ge(d_h[s % 2], 16 * (s // 2 + 1))
                            dve.tensor_tensor(h[0:HP, s % 2, 0:2, :],
                                              pa[0:HP, 0, :].rearrange("p (c d) -> p c d", c=2), posb[0:HP, :, :],
                                              ALU.add).then_inc(c_h, 1)
                            dve.wait_ge(c_h, s + 1)
                            normalise(h[:, s % 2, :, :], st, mv, s + 1, c_xh, rs, xh, c_st, c_mv, c_rs)
                        elif p == 2:
                            dve.wait_ge(M_QK, s + 1)
                            dve.tensor_tensor(qT[:, :, :], pa[:, 0:2, 0:S], dq, ALU.mult).then_inc(c_q, 1)
                            dve.tensor_tensor(kT[:, :, :], pa[:, 2:4, 0:S], dk, ALU.mult).then_inc(c_k, 1)
                        elif p == 3:
                            dve.wait_ge(c_v, s + 1)
                            dve.tensor_tensor(
                                kt[0:HP, :, :].rearrange("p c (h e) -> p c h e", h=HEADS),
                                pa[0:HP, 0:2, D:2 * D].rearrange("p c (h e) -> p c h e", h=HEADS),
                                kd[0:HP, :, :].unsqueeze(3).broadcast_to([HP, 2, HEADS, HD]), ALU.mult)\
                                .then_inc(c_kt, 1)
                        elif p == 4:
                            dve.wait_ge(M_GS, s + 1)
                            dve.tensor_tensor(sbd[:, :, :, :].rearrange("p h u e -> p (h u) e"),
                                              pa[:, 0, :].rearrange("p (k e) -> p k e", k=4),
                                              bd.unsqueeze(1).broadcast_to([P, 4, P]), ALU.mult).then_inc(c_state, 1)
                            dve.wait_ge(c_th, s + 1)
                            dve.scalar_tensor_tensor(s2[:, :, :], th[:, :, :], 1.0, pa[:, 2:4, 0:S], ALU.add, ALU.mult)\
                                .then_inc(c_s2, 1)
                        elif p == 5:
                            dve.wait_ge(M_SA, s + 1)
                            score_mask(s, 0, 0)
                            score_mask(s, 1, 1).then_inc(c_scA, 1)
                        elif p == 6:
                            dve.wait_ge(M_SB, s + 1)
                            score_mask(s, 2, 0).then_inc(c_scB, 1)
                        elif p == 7:
                            dve.wait_ge(c_sq, s + 1)
                            dve.tensor_reduce(ss[:, :], sq[:, :, :].rearrange("p c (h e) -> p (c h) e", h=HEADS),
                                              AX.X, ALU.add).then_inc(c_ss, 1)
                            dve.wait_ge(c_rg, s + 1)
                            r = rg[:, :].rearrange("p (c h) -> p c h", c=3)
                            dve.tensor_tensor(
                                rn[0:HP, 0:2, :].rearrange("p c (h e) -> p (c h) e", h=HEADS),
                                pa[0:HP, 0, :].rearrange("p (k e) -> p k e", e=HD),
                                rg[0:HP, 0:2 * HEADS].unsqueeze(2).broadcast_to([HP, 2 * HEADS, HD]), ALU.mult)
                            dve.tensor_tensor(
                                rn[:, 2, :].rearrange("p (h e) -> p h e", h=HEADS),
                                pa[:, 1, 0:D].rearrange("p (h e) -> p h e", h=HEADS),
                                rg[:, 2 * HEADS:3 * HEADS].unsqueeze(2).broadcast_to([P, HEADS, HD]), ALU.mult)\
                                .then_inc(c_rn, 1)
                        elif p == 8:
                            dve.wait_ge(M_RT, s + 1)
                            dve.wait_ge(c_s2b, s + 1)
                            for hf in range(DH):
                                last = dve.scalar_tensor_tensor(oT[:, hf, :], pa[:, 2 + hf, 0:S], gn[:, 0, hf:hf + 1],
                                                                s2b[:, hf, :], ALU.mult, ALU.add)
                            last.then_inc(c_oT, 1)
                        elif p == 9:
                            dve.wait_ge(M_W2, s + 1)
                            if s >= 2:
                                dve.wait_ge(d_out[s % 2], 32 * (s // 2))
                            dve.tensor_tensor(h2[0:HP, s % 2, 0:2, :],
                                              pa[0:HP, 0, :].rearrange("p (c d) -> p c d", c=2),
                                              h[0:HP, s % 2, 0:2, :], ALU.add)
                            dve.tensor_tensor(h2[:, s % 2, 2, :], pa[:, 1, 0:D], h[:, s % 2, 2, :], ALU.add)\
                                .then_inc(c_h2, 1)
                            dve.wait_ge(c_h2, s + 1)
                            if s:
                                dve.wait_ge(c_hi, s)
                                dve.wait_ge(c_lo, s)
                            normalise(h2[:, s % 2, :, :], st2, mv2, s + 1, c_xs, rs2x, xs, c_st2, c_mv2, c_rs2x)
                        elif p == 11:
                            dve.wait_ge(M_RTR, s + 1)
                            dve.tensor_copy(lg[:, :, :, s], pa[:, 0, 0:3 * NE].rearrange("p (c e) -> p c e", c=3))\
                                .then_inc(c_lg, 1)

                    def softmax():
                        dve.wait_ge(c_lg, G)
                        over = lg[:, :, :, :].rearrange("p c e s -> p c s e")
                        dve.tensor_reduce(lmax[:, :, :], over, AX.X, ALU.max).then_inc(c_soft, 1)
                        dve.wait_ge(c_soft, 1)
                        dve.tensor_tensor(ldif[:, :, :, :], lg[:, :, :, :],
                                          lmax[:, :, :].unsqueeze(2).broadcast_to([P, 3, NE, G]), ALU.subtract)\
                            .then_inc(c_soft, 1)
                        dve.wait_ge(c_exp, 1)
                        dve.tensor_reduce(lsum[:, :, :], lexp[:, :, :, :].rearrange("p c e s -> p c s e"), AX.X, ALU.add)\
                            .then_inc(c_soft, 1)
                        dve.wait_ge(c_soft, 3)
                        dve.reciprocal(lrec[:, :, :], lsum[:, :, :]).then_inc(c_soft, 1)
                        dve.wait_ge(c_soft, 4)
                        dve.tensor_tensor(prob[:, :, :, :], lexp[:, :, :, :],
                                          lrec[:, :, :].unsqueeze(2).broadcast_to([P, 3, NE, G]), ALU.mult)\
                            .then_inc(c_prob, 1)

                    def choose(r):
                        if r < 0:
                            dve.wait_ge(m_pT, 1)
                            dve.tensor_copy(val[:, 0, 0:S], pa[0:ROWS, 1, 0:S]).then_inc(c_val, 1)
                            dve.wait_ge(c_val, 1)
                        else:
                            k = slice(8 * r, 8 * r + 8)
                            src, dst = val[:, 0 if r == 0 else 1, :], val[:, 1, :]
                            dve.max(top[:, k], src).then_inc(c_top, 1)
                            dve.wait_ge(c_top, 3 * r + 1)
                            dve.max_index(topi[:, k], top[:, k], src).then_inc(c_top, 1)
                            dve.match_replace(dst, top[:, k], src, -1.0).then_inc(c_top, 1)
                            dve.wait_ge(c_top, 3 * r + 3)

                    def chosen():
                        dve.tensor_copy(idx16[:, 0:CAP], topi[:, NSENT:])
                        dve.tensor_copy(pack[:, :, 1], top[:, NSENT:]).then_inc(c_pick, 1)
                        dve.tensor_scalar(pack[:, :, 0].bitcast(U32), topi[:, NSENT:], rowbase, None, ALU.add)\
                            .then_inc(c_pick, 1)
                        dve.wait_ge(c_pick, 2)
                        dve.tensor_scalar(rowbase, rowbase, float(G * S), None, ALU.add)

                    def one_hot(s):
                        if s >= 2:
                            dve.wait_ge(m_g, 8 * (s - 1))
                        src = idxb[:, :, :].rearrange("p (e s) k -> p e s k", s=G)[:, :, s, :]
                        for c in range(3):
                            last = dve.tensor_scalar(sel[:, s % 2, c, :].rearrange("p (e k) -> p e k", k=PAD), src,
                                                     tok[:, c:c + 1], None, ALU.is_equal)
                        last.then_inc(c_sel, 1)

                    def gathered(s, half):
                        for k in range(4 * half + 1, 4 * half + 4, 2):
                            n = 8 * s + k
                            part, hf, quad = k // 4, k // 2 % 2, k % 2
                            dve.wait_ge(m_g, n + 1)
                            dve.tensor_copy(xin[:, part, hf, 4 * quad:4 * quad + 4, CAP * s:CAP * (s + 1)],
                                            pf[:, n % 4, 0:4 * CAP].rearrange("p (e k) -> p e k", k=CAP))\
                                .then_inc(c_g[1], 1)
                        if half and s + 2 < G:
                            one_hot(s + 2)

                    def split(e, f):
                        q = (FO * e + f) // 2
                        dve.wait_ge(c_hh, q + 1)
                        dve.scalar_tensor_tensor(h1[:, e % 2, 1, f - 1:f + 1, :], h1f[:, q % 2, :, :], wsc[:, e, 1:2],
                                                 h1[:, e % 2, 0, f - 1:f + 1, :], ALU.mult, ALU.subtract)\
                            .then_inc(c_hl, 1)

                    def prepare_scale(e):
                        dve.wait_ge(d_w[0], 32 * (e + 1))
                        dve.tensor_reduce(am[:, 0:1], wst2[:, 0:DH * FF], AX.X, ALU.max, apply_absolute_value=True)
                        dve.tensor_reduce(am[:, 1:2], wst2[:, DH * FF:WP], AX.X, ALU.max, apply_absolute_value=True)\
                            .then_inc(p_am, 1)
                        dve.wait_ge(p_amr, e + 1)
                        n = 4 * e
                        if e:
                            dve.wait_ge(p_hi, e)
                        dve.tensor_scalar(amc[:, :], amr[:, :], 1e-18, None, ALU.max).then_inc(p_sc, 1)
                        dve.wait_ge(p_sc, n + 1)
                        dve.tensor_scalar(pw[:, :].bitcast(I32), amc[:, :].bitcast(I32), 0x7F800000, None,
                                          ALU.bitwise_and).then_inc(p_sc, 1)
                        dve.wait_ge(p_sc, n + 2)
                        dve.reciprocal(pinv[:, :], pw[:, :]).then_inc(p_sc, 1)
                        dve.wait_ge(p_sc, n + 3)
                        dve.tensor_scalar(wscale[:, :], pinv[:, :], 2.0 ** 14, None, ALU.mult)
                        dve.tensor_scalar(wsc[:, e, 0:1], pw[:, 0:1], 2.0 ** -14 / XS, None, ALU.mult)
                        dve.tensor_scalar(wsc[:, e, 1:2], pinv[:, 0:1], 2.0 ** 6, None, ALU.mult)
                        dve.scalar_tensor_tensor(wsc[:, e, 2:3], pw[:, 0:1], 2.0 ** -20, pw[:, 1:2], ALU.mult, ALU.mult)\
                            .then_inc(p_sc, 1)

                    def prepare_split(e):
                        dve.wait_ge(p_sc, 4 * e + 4)
                        dve.wait_ge(p_hi, e + 1)
                        for k in range(2):
                            sl = slice(0, DH * FF) if k == 0 else slice(DH * FF, WP)
                            last = dve.scalar_tensor_tensor(wr[:, e % 2, 1, sl], wst2[:, sl], wscale[:, k:k + 1],
                                                            wr[:, e % 2, 0, sl], ALU.mult, ALU.subtract)
                        last.then_inc(p_lo, 1)

                    if experts:
                        dve.tensor_copy(slrow[:, :, :], slot[:, :, :, 0].bitcast(U32)).then_inc(c_slot, 1)
                        dve.tensor_tensor(gs[:, :, :], slot[:, :, :, 1],
                                          wsc[:, :, 2:3].broadcast_to([P, NE, 3]), ALU.mult).then_inc(c_slot, 1)
                        one_hot(0)
                        one_hot(1)
                    for step in steps:
                        if step[0] == "attn":
                            attention(*step[1:])
                        elif step[0] == "gather":
                            gathered(*step[1:])
                        elif step[0] == "mm1" and step[2] % 2:
                            split(*step[1:])
                        elif step[0] == "route":
                            softmax()
                        elif step[0] == "choose":
                            choose(step[1])
                        elif step[0] == "topk":
                            chosen()
                        elif step[0] == "prep_scale":
                            prepare_scale(step[1])
                        elif step[0] == "prep_split":
                            prepare_split(step[1])

                @block.gpsimd
                def _(pool):
                    def power(src, n, c_in, mid, c_mid, dst, c_out, width, mul):
                        pool.wait_ge(c_in, n)
                        pool.tensor_scalar(mid, src, mul, EPS, ALU.mult, ALU.add).then_inc(c_mid, 1)
                        pool.wait_ge(c_mid, n)
                        return pool.tensor_tensor(dst, mid, nhalf[:, 0:width], ALU.pow).then_inc(c_out, 1)

                    def attention(s, p):
                        if p == 0:
                            power(mv[:, :, 1], s + 1, c_mv, ve[:, :], c_ve, rs[:, :], c_rs, 3, 1.0)
                        elif p == 4:
                            pool.wait_ge(c_s2, s + 1)
                            for hf in range(DH):
                                last = pool.tensor_scalar(s2b[:, hf, :], s2[:, hf, :], gn[:, 1, hf:hf + 1], None, ALU.add)
                            last.then_inc(c_s2b, 1)
                        elif p == 7:
                            power(ss[:, :], s + 1, c_ss, ssb[:, :], c_ssb, rg[:, :], c_rg, 3 * HEADS, 1.0 / HD)
                        elif p == 9:
                            power(mv2[:, :, 1], s + 1, c_mv2, ve2[:, :], c_ve2, rs2[:, :], c_rs2, 3, 1.0)
                            pool.wait_ge(c_rs2, s + 1)
                            pool.tensor_scalar(rs2x[:, :], rs2[:, :], XS, 0.0, ALU.mult, ALU.add).then_inc(c_rs2x, 1)
                        elif p == 10:
                            pool.wait_ge(c_hi, s + 1)
                            pool.tensor_tensor(xhl[:, 1, s, :, :], xs[:, :, :], xhl[:, 0, s, :, :], ALU.subtract)\
                                .then_inc(c_lo, 1)

                    for step in steps:
                        if step[0] == "attn":
                            attention(*step[1:])
                        elif step[0] == "mm2" and step[2:] == (2, 1):
                            e = step[1]
                            if e == 0:
                                pool.wait_ge(c_slot, 1)
                            pool.wait_ge(c_y, 3 * e + 3)
                            if e:
                                pool.wait_ge(d_scat, 48 * e)
                            for c, (k0, n) in enumerate(SC):
                                pool.indirect_dma_start(
                                    out=out_rows, out_offset=bass.IndirectOffsetOnAxis(ap=slrow[0:n, e, c:c + 1], axis=0),
                                    in_=y[0:n, e % 2, c, :], in_offset=None, compute_op=ALU.add).then_inc(d_scat, 16)
                        elif step[0] == "prep_scale":
                            e = step[1]
                            pool.wait_ge(p_am, e + 1)
                            pool.partition_all_reduce(amr[:, :], am[:, :], P, RADD_MAX).then_inc(p_amr, 1)
                    if attend:
                        pool.wait_ge(c_lo, G)
                    if experts:
                        pool.wait_ge(d_scat, 48 * NE)
                        pool.dma_reset(range(d_scat.num, d_scat.num + 1))
            barrier()

        body(0, True, False, prepare=True)
        with nc.Fori(1, NG) as g:
            body(g, True, True)
        body(NG, False, True, more=False)


def constants():
    import numpy as np

    gamma = (1.0 - np.exp(np.linspace(np.log(1.0 / 512.0), np.log(1.0 / 32.0), HEADS))).astype(np.float32)
    gamma = gamma.astype(np.float64)
    t = np.zeros((P, C_ALL), np.float32)
    n, p = np.arange(S), np.arange(P)
    for hf in range(DH):
        per_row = gamma[HPH * hf + p // HD]
        t[:, C_DQ + S * hf:C_DQ + S * (hf + 1)] = per_row[:, None] ** n
        t[:, C_DK + S * hf:C_DK + S * (hf + 1)] = per_row[:, None] ** -n.astype(np.float64)
    for c in range(2):
        t[0:HP, C_KD + HEADS * c:C_KD + HEADS * (c + 1)] = gamma[None] ** -(HP * c + np.arange(HP, dtype=np.float64))[:, None]
    t[:, C_MASK:C_BD] = p[None] >= p[:, None]
    t[:, C_BD:C_ID] = p[None] // HD == p[:, None] // HD
    t[:, C_ID:C_TOK] = np.eye(P)
    for c, (t0, k) in enumerate(CH):
        t[:, C_TOK + c] = np.where(p < k, t0 + p, -1)
    t[0:ROWS, C_ROW] = S * (np.arange(ROWS) % G)
    return t


_INS = ["x", "txt", "L0_tok_W_embed", "L0_tok_b_embed", "L0_tok_pos_embed", "L0_attn_Wq", "L0_attn_Wk",
        "L0_attn_Wv", "L0_attn_W1", "L0_attn_W2", "L0_attn_gn_w", "L0_attn_gn_b", "L0_ffn_gate_w",
        "L0_ffn_w1", "L0_ffn_w2"]


def kernel(**inputs):
    import numpy as _np
    import concourse.bacc as _bacc
    from concourse import mybir as _mybir
    from concourse.bass_utils import run_bass_kernel_spmd as _run

    nc = _bacc.Bacc("TRN2", target_bir_lowering=False, num_devices=1)
    arrays, args = {}, []
    for name, a in [(n, inputs[n]) for n in _INS] + [("constants", constants())]:
        a = _np.ascontiguousarray(a)
        arrays[f"in_{name}_dram"] = a
        args.append(nc.dram_tensor(f"in_{name}_dram", a.shape, _mybir.dt.from_np(a.dtype), kind="ExternalInput").ap())
    args.append(nc.dram_tensor("out_dram", (B, S, D), F32, kind="ExternalOutput").ap())
    build(nc, *args)
    r = _run(nc, [arrays], core_ids=[0])
    return r.results[0]["out_dram"]
```

```python
from contextlib import ExitStack

import concourse.bass as bass
from concourse import mybir

F32 = mybir.dt.float32
F16 = mybir.dt.float16
U32 = mybir.dt.uint32
I32 = mybir.dt.int32
ALU = mybir.AluOpType
ACT = mybir.ActivationFunctionType
AX = mybir.AxisListType
RADD_MAX = bass.bass_isa.ReduceOp.max

P = 128
B = 32
SIDE, PATCH = 14, 16
CIN = 3
WPIX = SIDE * PATCH
NPATCH = SIDE * SIDE
NTXT = 128
S = NPATCH + NTXT
D = 256
DH = D // P
HEADS, HD = 8, 32
HPH = P // HD
HP = NPATCH // 2
CH = ((0, HP), (HP, HP), (NPATCH, NTXT))
NE, FF = 8, 1024
FO = FF // P
CAP = 2 * S // NE
G = 4
NG = B // G
SL = G * CAP
SC = ((0, 128), (128, 128), (256, SL - 256))
ROWS = NE * G
ROUNDS = (CAP + 7) // 8
NSENT = ROUNDS * 8 - CAP
RW = S + NSENT
EPS = 1e-5
JH = PATCH // 2
CI = CIN * PATCH
ES = CIN * PATCH * PATCH // P
EX = 2 * CI
LEFT = ES
XS = 2048.0
WP = DH * FF + FO * D
WH = DH * FF
NPH = 12

C_DQ = 0
C_DK = C_DQ + DH * S
C_KD = C_DK + DH * S
C_MASK = C_KD + 2 * HEADS
C_BD = C_MASK + P
C_ID = C_BD + P
C_ROW = C_ID + P
C_ALL = C_ROW + 1


GAP = (0, 3, 2, 4, 3, 4, 4, 4, 11, 5, 0, 3)
GAP_LAST = 12
GAP_ROUTE = 2
GAP_ROUND = 4
PREP_AT = ((0, "reduce"), (1, "scales"), (2, "hi"), (4, "lo"), (5, "reduce"), (7, "scales"), (7, "hi"), (9, "lo"))
COST = {"gather": 0.648, "mm1": 6 * 0.324, "mm2": 12 * 0.256}


def expert_steps():
    steps = [("gather", e, hf) for e in range(2) for hf in range(DH)] + [("mm1", 0, 0), ("mm1", 0, 1)]
    for e in range(NE):
        steps += [("mm1", e, f) for f in range(2, FO)]
        if e + 1 < NE:
            steps += [("mm1", e + 1, 0), ("mm1", e + 1, 1)]
        if e + 2 < NE:
            steps += [("gather", e + 2, hf) for hf in range(DH)]
        steps += [("mm2", e, c, half) for c in range(3) for half in range(2)]
    return steps


def plan(attend, experts, prepare):
    front = []
    if attend:
        front = [(GAP[0], ("attn", 0, 0))]
        for s in range(G):
            for p in range(1, NPH):
                front.append((GAP_LAST if (s, p) == (G - 1, 10) else GAP[p], ("attn", s, p)))
                if p == 9 and s + 1 < G:
                    front.append((0, ("attn", s + 1, 0)))
        front += [(GAP_ROUTE, ("route",)), (0, ("choose", -1))]
        front += [(GAP_ROUND, ("choose", r)) for r in range(ROUNDS)] + [(0, ("topk",))]
    back = []
    if experts:
        back = expert_steps()
    if prepare:
        where = {}
        for n in range(NE):
            for p, kind in PREP_AT[4 * (n % 2):4 * (n % 2) + 4]:
                where.setdefault((n // 2, p), []).append((kind, n))
    steps = []
    for gap, step in front:
        if prepare and step[0] == "attn":
            steps += where.get(step[1:], [])
        while experts and back and gap > 0:
            gap -= COST[back[0][0]]
            if gap < -2.5:
                break
            steps.append(back.pop(0))
        steps.append(step)
    return steps + back


def build(nc, x, txt, We, be, pos, Wq, Wk, Wv, W1, W2, gnw, gnb, gate, w1, w2, const, out):
    ctx = ExitStack()
    with ctx:
        def sb(name, shape, dt=F32):
            return ctx.enter_context(nc.sbuf_tensor(name, shape, dt))

        sems = []

        def sem(name):
            h = ctx.enter_context(nc.semaphore(name))
            sems.append(h)
            return h

        wscr = nc.dram_tensor("w_split", (NE, 2, P, WP), F16, kind="Internal").ap()
        scr_x = [nc.dram_tensor(f"x_split{k}", (G * S, 2 * D), F16, kind="Internal").ap() for k in range(2)]
        scr_slot = nc.dram_tensor("choice_slot", (ROWS * CAP, 2), F32, kind="Internal").ap()
        out_rows = out.rearrange("b s d -> (b s) d")

        cst = sb("cst", [P, C_ALL])
        dq = cst[:, C_DQ:C_DK].rearrange("p (h s) -> p h s", h=DH)
        dk = cst[:, C_DK:C_KD].rearrange("p (h s) -> p h s", h=DH)
        kd = cst[:, C_KD:C_MASK].rearrange("p (c h) -> p c h", c=2)
        mask = cst[:, C_MASK:C_BD]
        bd = cst[:, C_BD:C_ID]
        ident = cst[:, C_ID:C_ROW]
        rowbase = cst[0:ROWS, C_ROW:C_ALL]
        ident16 = sb("ident16", [P, P], F16)
        we = sb("we", [P, ES, D])
        posb = sb("posb", [P, 2, D])
        bebc = sb("bebc", [P, D])
        wqb = sb("wqb", [P, DH, P])
        wkvb = sb("wkvb", [P, DH, 2, P])
        wvraw = sb("wvraw", [P, DH, P])
        vsum = sb("vsum", [P, DH])
        w1g = sb("w1g", [P, DH, D])
        w2g = sb("w2g", [P, DH, D])
        gn = sb("gn", [P, 2, DH])
        gateT = sb("gateT", [P, DH, NE])
        nhalf = sb("nhalf", [P, 3 * HEADS])
        wsc = sb("wsc", [P, NE, 3])

        xt = sb("xt", [P, SIDE, WPIX])
        xe = sb("xe", [P, SIDE, WPIX])
        h = sb("h", [P, 2, 3, D])
        h2 = sb("h2", [P, 2, 3, D])
        st = sb("st", [P, 3, 6])
        mv = sb("mv", [P, 3, 2])
        ve = sb("ve", [P, 3])
        rs = sb("rs", [P, 3])
        xh = sb("xh", [P, 3, D])
        x2T = sb("x2T", [P, DH, 3 * P])
        xT = x2T[:, :, 0:S]
        qT = sb("qT", [P, DH, S])
        kT = sb("kT", [P, DH, S])
        kt = sb("kt", [P, 2, D])
        v = sb("v", [P, 3, D])
        s2 = sb("s2", [P, DH, S])
        s2b = s2
        sbd = sb("sbd", [P, DH, 2, P])
        sc = sb("sc", [P, 3, HEADS, P])
        sq = sb("sq", [P, 3, D])
        ss = sb("ss", [P, 3 * HEADS])
        ssb = sb("ssb", [P, 3 * HEADS])
        rg = sb("rg", [P, 3 * HEADS])
        rn = xh
        oT = sb("oT", [P, DH, S])
        th = oT
        st2 = sb("st2", [P, 3, 6])
        mv2 = sb("mv2", [P, 3, 2])
        ve2 = sb("ve2", [P, 3])
        rs2 = sb("rs2", [P, 3])
        rs2x = sb("rs2x", [P, 3])
        xs = sb("xs", [P, 3, D])
        lg = sb("lg", [P, 3, NE, G])
        lmax = sb("lmax", [P, 3, G])
        ldif = sb("ldif", [P, 3, NE, G])
        lexp = sb("lexp", [P, 3, NE, G])
        lsum = sb("lsum", [P, 3, G])
        lrec = sb("lrec", [P, 3, G])
        prob = sb("prob", [P, 3, NE, G])
        val = sb("val", [ROWS, 2, RW])
        top = sb("top", [ROWS, ROUNDS * 8])
        topi = sb("topi", [ROWS, ROUNDS * 8], U32)
        pack = sb("pack", [ROWS, CAP, 2])

        xhl = sb("xhl", [P, 2, 3, 2, D], F16)

        slot = sb("slot", [P, NE, 3, 2])

        slrow = sb("slrow", [P, NE, 3], U32)
        slout = sb("slout", [P, NE, 3], U32)
        base = sb("base", [P, 1])
        gs = sb("gs", [P, NE, 3])
        n_y, n_xg, n_xin = 2 * 3 * D, 3 * 2 * D, 2 * DH * SL
        ring = sb("ring", [P, n_y + n_xg + n_xin])
        y = ring[:, 0:n_y].rearrange("p (b c d) -> p b c d", b=2, c=3)
        xg = ring[:, n_y:n_y + n_xg].bitcast(F16).rearrange("p (b c d) -> p b c d", b=2, c=3)
        xin = ring[:, n_y + n_xg:].bitcast(F16).rearrange("p (b h k n) -> p b h k n", b=2, h=DH, k=2)
        wr = sb("wr", [P, 2, 2, 2, WH], F16)
        h1f = sb("h1f", [P, 2, 2, SL])
        h1 = sb("h1", [P, 2, 2, FO, SL], F16)

        raw = [t.rearrange("p (k w) -> p k w", k=2) for t in
               (ring[:, 0:WP], h1[:, :, :, :, :].rearrange("p a b c d -> p (a b c d)").bitcast(F32)[:, 0:WP])]
        am = sb("am", [P, 2])
        amr = sb("amr", [P, 2])
        amc = sb("amc", [P, 2])
        pw = sb("pw", [P, 2])
        pinv = sb("pinv", [P, 2])
        wscale = sb("wscale", [P, 2])

        pa = ctx.enter_context(nc.psum_tensor("pa", [P, 4, 512], F32))
        pf = ctx.enter_context(nc.psum_tensor("pf", [P, 4, 512], F32))
        turned = pf[:, 0:2, 0:SL].bitcast(F16).rearrange("p b (k n) -> p b k n", k=2)

        d_x, d_h = sem("d_x"), [sem("d_txt0"), sem("d_txt1")]
        d_w = [[sem(f"d_w{k + 1}_{e}") for e in ("even", "odd")] for k in range(2)]
        d_raw = [sem("d_raw0"), sem("d_raw1")]
        d_out = [sem("d_out0"), sem("d_out1")]
        d_c2, d_tail = sem("d_slot_out"), sem("d_slot_in")
        d_xh = [sem("d_xh0"), sem("d_xh1")]
        d_scat, d_gath = sem("d_scatter"), [sem("d_gather0"), sem("d_gather1")]
        d_setup, c_xe = sem("d_setup"), sem("c_xe")
        names = ("embed", "xT", "qk", "vk", "gated_state", "scoresA", "scoresB", "ret", "retT", "w2", "x2T", "router")
        mm = [sem("mm_" + n) for n in names]
        (M_EMB, M_XT, M_QK, M_VK, M_GS, M_SA, M_SB, M_RET, M_RT, M_W2, M_X2T, M_RTR) = mm
        c_h, c_st, c_mv, c_ve, c_rs, c_xh = (sem("c_" + n) for n in ("h", "st", "mv", "ve", "rs", "xh"))
        c_xT, c_q, c_k, c_v, c_kt, c_th, c_s2, c_s2b, c_state = (
            sem("c_" + n) for n in ("xT", "q", "k", "v", "kt", "th", "s2", "s2b", "state"))
        c_scA, c_scB, c_sq, c_ss, c_ssb, c_rg, c_rn, c_oT, c_h2 = (
            sem("c_" + n) for n in ("scA", "scB", "sq", "ss", "ssb", "rg", "rn", "oT", "h2"))
        c_st2, c_mv2, c_ve2, c_rs2, c_rs2x, c_xs, c_hi, c_lo, c_x2T, c_lg = (
            sem("c_" + n) for n in ("st2", "mv2", "ve2", "rs2", "rs2x", "xs", "hi", "lo", "x2T", "lg"))
        c_soft, c_exp, c_prob, m_pT, c_val, c_top, c_pick = (
            sem("c_" + n) for n in ("soft", "exp", "prob", "pT", "val", "top", "pick"))
        m_g, c_g, c_slot = sem("mm_gather"), sem("c_gather"), sem("c_slot")
        m_1, m_2, c_gelu, c_hh, c_hl, c_y = (sem(n) for n in ("mm_1", "mm_2", "c_gelu", "c_hh", "c_hl", "c_y"))
        p_am, p_amr, p_sc, p_hi, p_lo = (sem("p_" + n) for n in ("am", "amr", "sc", "hi", "lo"))
        p_out = [sem("p_out0"), sem("p_out1")]
        s_init, s_v, s_pool = sem("s_init"), sem("s_v"), sem("s_pool")

        def barrier():
            nc.sync.sem_clear(range(sems[0].num, sems[-1].num + 1))
            nc.all_engine_barrier(sem_only=True)

        def patches(t, j, c):
            rows = SIDE // 2
            return t[:, rows * c:rows * (c + 1), :].rearrange("p a (b j) -> p a b j", j=PATCH)[:, :, :, j]

        def load_image(sp, i, s):
            def rows(c, shift):
                return x[i, c].rearrange("(a i) w -> i a w", i=PATCH)[:, :, shift:WPIX]
            for half in range(2):
                for c in range(CIN):
                    q = CI * half + PATCH * c
                    sp.dma_start(xt[q:q + PATCH, :, 0:WPIX - JH * half], rows(c, JH * half)).then_inc(d_x, 16)
                q = EX + PATCH * half
                sp.dma_start(xt[q:q + PATCH, :, :], rows(half, 0)).then_inc(d_x, 16)
                sp.dma_start(xe[q:q + PATCH, :, 0:WPIX - JH * half], rows(2, JH * half)).then_inc(d_x, 16)
            sp.dma_start(h[:, s % 2, 2, :], txt[i]).then_inc(d_h[s % 2], 16)
        n_x = 16 * 2 * (CIN + 2)

        def take_left(act):
            def col(t, j):
                return t[EX:P, :, :].rearrange("p a (b j) -> p a b j", j=PATCH)[:, :, :, j:j + 2]
            act.copy(col(xt, 0), col(xt, LEFT))
            act.copy(col(xt, 2), col(xt, JH + LEFT))
            act.copy(col(xt, 4), col(xe, LEFT)).then_inc(c_xe, 1)

        with nc.Block(no_gpsimd_drain=True) as block:
            @block.sync
            def _(sp):
                sp.dma_start(cst[:, :], const).then_inc(d_setup, 16)
                sp.dma_start(posb[0:HP, :, :], pos[0].rearrange("(c p) d -> p c d", c=2)).then_inc(d_setup, 16)
                sp.dma_start(bebc[:, :], be.partition_broadcast(P)).then_inc(d_setup, 16)
                sp.dma_start(w1g[:, :, :], W1.rearrange("(h p) d -> p h d", h=DH)).then_inc(d_setup, 16)
                sp.dma_start(w2g[:, :, :], W2.rearrange("(h p) d -> p h d", h=DH)).then_inc(d_setup, 16)
                with nc.allow_non_contiguous_dma(reason="a few hundred words, once"):
                    sp.dma_start(gn[:, 0, :], gnw.rearrange("(h p) -> p h", h=DH)).then_inc(d_setup, 16)
                    sp.dma_start(gn[:, 1, :], gnb.rearrange("(h p) -> p h", h=DH)).then_inc(d_setup, 16)
                    for hf in range(DH):
                        sp.dma_start(gateT[:, hf, :], gate[:, hf * P:(hf + 1) * P].rearrange("e p -> p e"))\
                            .then_inc(d_setup, 16)
                rows = We.rearrange("(k j) e -> k j e", j=PATCH)
                two = slice(2 * PATCH, 3 * PATCH)
                for half in range(2):
                    j, q = JH * half, EX + PATCH * half
                    sp.dma_start(we[CI * half:CI * (half + 1), :, :], rows[:, j:j + ES, :]).then_inc(d_setup, 16)
                    sp.dma_start(we[EX:P, 2 * half:2 * half + 2, :], rows[0:P - EX, j + LEFT:j + JH, :])\
                        .then_inc(d_setup, 16)
                    sp.dma_start(we[q:q + PATCH, 4:6, :], rows[two, j + LEFT:j + JH, :]).then_inc(d_setup, 16)
                load_image(sp, 0, 0)
                sp.wait_ge(d_x, n_x)
                sp.wait_ge(d_h[0], 16)
            n_setup = 16 * (9 + 6 + 3 * HPH)

            @block.scalar
            def _(act):
                act.wait_ge(s_init, 3)
                for r in range(HPH):
                    a = slice(HD * r, HD * (r + 1))
                    for dst, w in ((wqb[a, :, a], Wq), (wkvb[a, :, 1, a], Wk), (wvraw[a, :, a], Wv)):
                        act.dma_start(dst, w.rearrange("(h r) d e -> r d h e", h=DH)[r]).then_inc(d_setup, 16)
                act.wait_ge(d_x, n_x)
                take_left(act)

            @block.gpsimd
            def _(pool):
                pool.memset(slot[:, :, :, :], 0.0).then_inc(s_pool, 1)
                pool.wait_ge(s_pool, 1)

            @block.vector
            def _(dve):
                dve.memset(wqb[:, :, :], 0.0).then_inc(s_init, 1)
                dve.memset(wkvb[:, :, :, :], 0.0).then_inc(s_init, 1)
                dve.memset(wvraw[:, :, :], 0.0).then_inc(s_init, 1)
                dve.memset(h[:, :, 0:2, :], 0.0)
                dve.memset(h2[:, :, :, :], 0.0)
                dve.memset(sq[:, :, :], 0.0)
                dve.memset(nhalf[:, :], -0.5)
                dve.memset(base[:, :], 0.0)
                for k in range(NSENT):
                    dve.memset(val[:, 0, S + k:S + k + 1], 2.0 + k)
                dve.wait_ge(d_setup, n_setup)
                dve.tensor_copy(ident16[:, :], ident)
                dve.tensor_tensor(posb[0:HP, :, :], posb[0:HP, :, :],
                                  bebc[0:HP, :].unsqueeze(1).broadcast_to([HP, 2, D]), ALU.add)
                dve.tensor_scalar(gn[:, :, :], gn[:, :, :], 2.0, None, ALU.mult)
                dve.tensor_scalar(w2g[:, :, :], w2g[:, :, :], 0.5, None, ALU.mult)
                dve.tensor_reduce(vsum[:, :], wvraw[:, :, :], AX.X, ALU.add).then_inc(s_v, 1)
                dve.wait_ge(s_v, 1)
                dve.tensor_scalar(vsum[:, :], vsum[:, :], -1.0 / HD, None, ALU.mult).then_inc(s_v, 1)
                dve.wait_ge(s_v, 2)
                for hf in range(DH):
                    dve.scalar_tensor_tensor(wkvb[:, hf, 0, :], wvraw[:, hf, :], vsum[:, hf:hf + 1], bd,
                                             ALU.add, ALU.mult)
        barrier()

        def body(g, parity, attend, experts, prepare=False, more=True, ahead=True):
            steps = plan(attend, experts, prepare)

            def img(s):
                return g * G + s

            with nc.Block(no_gpsimd_drain=True) as block:
                @block.sync
                def _(sp):
                    def load_weights(e, k):
                        sp.dma_start(wr[:, e % 2, k, :, :].rearrange("p a b -> p (a b)"), wscr[e, k])\
                            .then_inc(d_w[k][e % 2], 16)

                    def load_raw(n):
                        e = (n + 1) % NE
                        sp.dma_start(raw[n % 2][:, 0, :].rearrange("p (h f) -> p h f", h=DH),
                                     w1[e].rearrange("(h p) f -> p h f", h=DH)).then_inc(d_raw[n % 2], 16)
                        sp.dma_start(raw[n % 2][:, 1, :].rearrange("p (o d) -> p o d", o=FO),
                                     w2[e].rearrange("(o p) d -> p o d", o=FO)).then_inc(d_raw[n % 2], 16)

                    if prepare:
                        load_raw(0)
                        load_raw(1)
                    if experts:
                        load_weights(1, 0)
                        load_weights(1, 1)
                    for step in steps:
                        if step[0] == "attn" and step[2] == 0 and (ahead or step[1] + 1 < G):
                            s = step[1] + 1
                            sp.wait_ge(M_EMB, s)
                            if s >= 2:
                                sp.wait_ge(c_h2, s - 1)
                            load_image(sp, img(s), s)
                        if step[0] == "attn" and step[2] == 10:
                            s = step[1]
                            sp.wait_ge(c_hi, s + 1)
                            sp.wait_ge(c_lo, s + 1)
                            rows = scr_x[parity].rearrange("(g s) d -> g s d", g=G)[s]
                            sp.dma_start(rows[0:NPATCH].rearrange("(c p) d -> p c d", c=2),
                                         xhl[0:HP, s % 2, 0:2, :, :].rearrange("p c k d -> p c (k d)"))\
                                .then_inc(d_xh[s % 2], 16)
                            sp.dma_start(rows[NPATCH:S],
                                         xhl[:, s % 2, 2, :, :].rearrange("p k d -> p (k d)")).then_inc(d_xh[s % 2], 16)
                        if step[0] == "attn" and step[2] == 9:
                            s = step[1]
                            sp.wait_ge(c_h2, s + 1)
                            rows = out[img(s)]
                            sp.dma_start(rows[0:NPATCH].rearrange("(c p) d -> p c d", c=2), h2[0:HP, s % 2, 0:2, :])\
                                .then_inc(d_out[s % 2], 16)
                            sp.dma_start(rows[NPATCH:S], h2[:, s % 2, 2, :]).then_inc(d_out[s % 2], 16)
                        last1 = step[0] == "mm1" and step[2] == FO - 1
                        last2 = step[0] == "mm2" and step[2:] == (2, 1)
                        if last1 or last2:
                            e = step[1]
                            if e + 2 < NE or (e + 2 == NE and more):
                                if last1:
                                    sp.wait_ge(m_1, FO * (e + 1))
                                else:
                                    sp.wait_ge(m_2, 3 * (e + 1))
                                load_weights((e + 2) % NE, int(last2))
                        if step[0] == "topk":
                            sp.wait_ge(c_pick, 2)
                            sp.dma_start(scr_slot.rearrange("(r k) t -> r (k t)", r=ROWS),
                                         pack[:, :, :].rearrange("r k t -> r (k t)")).then_inc(d_c2, 16)
                            sp.wait_ge(d_c2, 16)
                            if experts:
                                sp.wait_ge(c_slot, 3)
                            per = scr_slot.rearrange("(e k) t -> e k t", e=NE)
                            with nc.allow_non_contiguous_dma(reason="two words per slot"):
                                for c, (k0, n) in enumerate(SC):
                                    sp.dma_start(slot[0:n, :, c, :], per[:, k0:k0 + n, :].rearrange("e k t -> k e t"))\
                                        .then_inc(d_tail, 16)
                        if step[0] == "lo":
                            n = step[1]
                            e = (n + 1) % NE
                            sp.wait_ge(p_hi, n + 1)
                            sp.wait_ge(p_lo, n + 1)
                            if n + 2 < NE:
                                load_raw(n + 2)
                            for k in range(2):
                                sp.dma_start(wscr[e, k], wr[:, e % 2, k, :, :].rearrange("p a b -> p (a b)"))\
                                    .then_inc(p_out[e % 2], 16)
                    if prepare:
                        for k in range(2):
                            sp.wait_ge(p_out[k], 32 * (NE // 2))
                    if attend:
                        for k in range(2):
                            sp.wait_ge(d_out[k], 32 * (G // 2))
                            sp.wait_ge(d_xh[k], 32 * (G // 2))
                        sp.wait_ge(d_tail, 16 * 3)
                    if attend and ahead:
                        sp.wait_ge(d_x, n_x * G)
                        sp.wait_ge(d_h[0], 16 * (G // 2))
                    if experts and more:
                        for k in range(2):
                            sp.wait_ge(d_w[k][0], 16 * (NE // 2))

                @block.tensor
                def _(pe):
                    def embed(s):
                        if s:
                            pe.wait_ge(d_x, n_x * s)
                            pe.wait_ge(c_xe, s)
                            pe.wait_ge(c_oT, s)
                        for c in range(2):
                            for j in range(ES):
                                last = pe.matmul(pa[0:HP, 2, D * c:D * (c + 1)], patches(xt, j, c), we[:, j, :],
                                                 start=j == 0, stop=j == ES - 1)
                        last.then_inc(M_EMB, 1)

                    def turn(src, bank, pad):
                        for hf in range(DH):
                            for c, (t0, n) in enumerate(CH):
                                n, t0 = (P, P * c) if pad else (n, t0)
                                last = pe.transpose(pa[:, bank + hf, t0:t0 + n], src[0:n, c, P * hf:P * (hf + 1)],
                                                    ident[0:n, 0:n])
                        return last

                    def project_qk(s):
                        pe.wait_ge(c_xT, s + 1)
                        if s:
                            pe.wait_ge(c_lg, s)
                        for k in range(2):
                            for hf in range(DH):
                                lhs = wqb[:, hf, :] if k == 0 else wkvb[:, hf, 1, :]
                                last = pe.matmul(pa[:, 2 * k + hf, 0:S], lhs, xT[:, hf, :], start=True, stop=True)
                        last.then_inc(M_QK, 1)

                    def project_vk(s):
                        pe.wait_ge(c_q, s + 1)
                        for c, (t0, n) in enumerate(CH):
                            if c == 2:
                                pe.wait_ge(c_k, s + 1)
                            w = 2 if c < 2 else 1
                            bank = pa[0:n, c, :].rearrange("p (w h e) -> p w h e", w=2, h=DH)
                            for hf in range(DH):
                                last = pe.matmul(bank[:, 0:w, hf, :], xT[:, hf, t0:t0 + n], wkvb[:, hf, 0:w, :],
                                                 start=hf == 0, stop=True, skip_group_check=True)
                        last.then_inc(M_VK, 1)

                    def gated_state(s):
                        for m in (1, 0):
                            if m == 0:
                                pe.wait_ge(c_v, s + 1)
                            for hf in range(DH):
                                pe.matmul(pa[:, 2 + m, 0:S], w1g[:, hf, P * m:P * (m + 1)], xT[:, hf, :],
                                          start=hf == 0, stop=hf == DH - 1)
                        pe.wait_ge(c_kt, s + 1)
                        for hf in range(DH):
                            for upto in range(2):
                                o = P * (2 * hf + upto)
                                for c in range(upto + 1):
                                    last = pe.matmul(pa[:, 0, o:o + P], kt[0:HP, c, P * hf:P * (hf + 1)],
                                                     v[0:HP, c, P * hf:P * (hf + 1)], start=c == 0, stop=c == upto)
                        last.then_inc(M_GS, 1)

                    def scores(c, place):
                        t0, n = CH[c]
                        for head in range(HEADS):
                            hf, r = head // HPH, head % HPH
                            a = slice(HD * r, HD * (r + 1))
                            o = 256 * place + P * hf
                            last = pe.matmul(pa[0:n, r, o:o + n], kT[a, hf, t0:t0 + n], qT[a, hf, t0:t0 + n],
                                             start=True, stop=True)
                        return last

                    def retain(s):
                        pe.wait_ge(c_scB, s + 1)
                        for c, (t0, n) in enumerate(CH):
                            o, bank = (D * c, 0) if c < 2 else (0, 1)
                            if c:
                                for hf in range(DH):
                                    pe.matmul(pa[0:n, bank, o + P * hf:o + P * (hf + 1)], qT[:, hf, t0:t0 + n],
                                              sbd[:, hf, c - 1, :], start=hf == 0, stop=False, skip_group_check=True)
                            for head in range(HEADS):
                                a = slice(HD * head, HD * (head + 1))
                                last = pe.matmul(pa[0:n, bank, o + HD * head:o + HD * (head + 1)],
                                                 sc[0:n, c, head, 0:n], v[0:n, c, a],
                                                 start=c == 0 and head == 0, stop=True, skip_group_check=True)
                        last.then_inc(M_RET, 1)

                    def mix(s):
                        pe.wait_ge(c_oT, s + 1)
                        for c, (t0, n) in enumerate(CH):
                            o, bank = (D * c, 0) if c < 2 else (0, 1)
                            for hf in range(DH):
                                last = pe.matmul(pa[0:n, bank, o:o + D], oT[:, hf, t0:t0 + n], w2g[:, hf, :],
                                                 start=hf == 0, stop=hf == DH - 1)
                        last.then_inc(M_W2, 1)

                    def attention(s, p):
                        if p == 0:
                            embed(s)
                        elif p == 1:
                            pe.wait_ge(c_xh, s + 1)
                            turn(xh, 1, False).then_inc(M_XT, 1)
                        elif p == 2:
                            project_qk(s)
                        elif p == 3:
                            project_vk(s)
                        elif p == 4:
                            gated_state(s)
                        elif p == 5:
                            pe.wait_ge(c_s2, s + 1)
                            pe.wait_ge(c_state, s + 1)
                            scores(0, 0)
                            scores(1, 1).then_inc(M_SA, 1)
                        elif p == 6:
                            pe.wait_ge(c_scA, s + 1)
                            scores(2, 0).then_inc(M_SB, 1)
                        elif p == 7:
                            retain(s)
                        elif p == 8:
                            pe.wait_ge(c_rn, s + 1)
                            turn(rn, 2, False).then_inc(M_RT, 1)
                        elif p == 9:
                            mix(s)
                        elif p == 10:
                            pe.wait_ge(c_xs, s + 1)
                            turn(xs, 0, True).then_inc(M_X2T, 1)
                        elif p == 11:
                            pe.wait_ge(c_x2T, s + 1)
                            for c in range(3):
                                for hf in range(DH):
                                    last = pe.matmul(pa[:, 3, NE * c:NE * (c + 1)], x2T[:, hf, P * c:P * (c + 1)],
                                                     gateT[:, hf, :], start=hf == 0, stop=hf == DH - 1)
                            last.then_inc(M_RTR, 1)

                    def gather(e, hf):
                        if hf == 0:
                            pe.wait_ge(d_gath[e % 2], 48 * (e // 2 + 1))
                        if e == 1:
                            pe.wait_ge(c_g, hf + 1)
                        elif e:
                            pe.wait_ge(c_gelu, FO * (e - 1) + hf + 1)
                        for part in range(2):
                            for c, (k0, n) in enumerate(SC):
                                o = D * part + P * hf
                                last = pe.transpose(turned[:, hf, part, k0:k0 + n], xg[0:n, e % 2, c, o:o + P],
                                                    ident16[0:n, 0:n])
                        last.then_inc(m_g, 1)

                    def first(e, f):
                        m = FO * e + f
                        if f == 0:
                            pe.wait_ge(c_g, DH * (e + 1))
                        if e == 0 and f < 2:
                            pe.wait_ge(c_g, DH + f + 1)
                        elif f in (2, 3) and 0 < e < NE - 1:
                            pe.wait_ge(c_g, DH * (e + 1) + f - 1)
                        if f == 0 and e:
                            pe.wait_ge(d_w[0][e % 2], 16 * ((e + 1) // 2))
                        if m >= 2:
                            pe.wait_ge(c_gelu, m - 1)
                        k = 0
                        for hf in range(DH):
                            for wp, xp in ((0, 0), (1, 0), (0, 1)):
                                o = FF * hf + P * f
                                last = pe.matmul(pf[:, m % 2, 0:SL], wr[:, e % 2, 0, wp, o:o + P], xin[:, e % 2, hf, xp, :],
                                                 start=k == 0, stop=k == 5)
                                k += 1
                        last.then_inc(m_1, 1)

                    def second(e, c, half):
                        k0, n = SC[c]
                        if c == 0 and half == 0:
                            if e:
                                pe.wait_ge(d_w[1][e % 2], 16 * ((e + 1) // 2))
                            pe.wait_ge(c_hl, 4 * e + 4)
                        if half == 0 and 3 * e + c >= 2:
                            pe.wait_ge(c_y, 3 * e + c - 1)
                        bank = 2 + (3 * e + c) % 2
                        k = 3 * FO // 2 * half
                        for f in range(FO // 2 * half, FO // 2 * (half + 1)):
                            for hp, wp in ((0, 0), (0, 1), (1, 0)):
                                o = D * f
                                last = pe.matmul(pf[0:n, bank, 0:D], h1[:, e % 2, hp, f, k0:k0 + n],
                                                 wr[:, e % 2, 1, wp, o:o + D], start=k == 0, stop=k == 3 * FO - 1)
                                k += 1
                        if half:
                            last.then_inc(m_2, 1)

                    for step in steps:
                        if step[0] == "attn":
                            attention(*step[1:])
                        elif step[0] == "gather":
                            gather(*step[1:])
                        elif step[0] == "mm1":
                            first(*step[1:])
                        elif step[0] == "mm2":
                            second(*step[1:])
                        elif step[0] == "route":
                            pe.wait_ge(c_prob, 1)
                            for c, (t0, n) in enumerate(CH):
                                last = pe.transpose(pa[0:ROWS, 1, t0:t0 + n],
                                                    prob[0:n, c, :, :].rearrange("p e s -> p (e s)"), ident[0:n, 0:n])
                            last.then_inc(m_pT, 1)

                @block.scalar
                def _(act):
                    def attention(s, p):
                        if p == 1:
                            act.wait_ge(M_XT, s + 1)
                            act.copy(xT[:, :, :], pa[:, 1:3, 0:S]).then_inc(c_xT, 1)
                        elif p == 3:
                            act.wait_ge(M_VK, s + 1)
                            act.copy(v[0:HP, 0:2, :], pa[0:HP, 0:2, 0:D])
                            act.copy(v[:, 2, :], pa[:, 2, 0:D]).then_inc(c_v, 1)
                        elif p == 4:
                            act.wait_ge(M_GS, s + 1)
                            act.activation(th[:, :, :], pa[:, 2:4, 0:S], ACT.Tanh, scale=0.5).then_inc(c_th, 1)
                        elif p == 5 and (ahead or s + 1 < G):
                            act.wait_ge(d_x, n_x * (s + 1))
                            take_left(act)
                        elif p == 7:
                            act.wait_ge(M_RET, s + 1)
                            act.square(sq[0:HP, 0:2, :], pa[0:HP, 0, :].rearrange("p (c d) -> p c d", c=2))
                            act.square(sq[:, 2, :], pa[:, 1, 0:D]).then_inc(c_sq, 1)
                        elif p == 10:
                            act.wait_ge(c_xs, s + 1)
                            if s >= 2:
                                act.wait_ge(d_xh[s % 2], 32 * (s // 2))
                            act.copy(xhl[:, s % 2, :, 0, :], xs[:, :, :]).then_inc(c_hi, 1)
                            act.wait_ge(M_X2T, s + 1)
                            act.copy(x2T[:, :, :], pa[:, 0:2, 0:3 * P]).then_inc(c_x2T, 1)

                    for step in steps:
                        if step[0] == "attn":
                            attention(*step[1:])
                        elif step[0] == "mm1":
                            e, f = step[1:]
                            m = FO * e + f
                            act.wait_ge(m_1, m + 1)
                            if m >= 4:
                                act.wait_ge(c_hl, m // 2 - 1)
                            act.activation(h1f[:, m // 2 % 2, m % 2, :], pf[:, m % 2, 0:SL], ACT.Gelu,
                                           scale=wsc[:, e, 0:1]).then_inc(c_gelu, 1)
                            if f % 2:
                                act.wait_ge(c_gelu, m + 1)
                                if f == 1 and e >= 2:
                                    act.wait_ge(m_2, 3 * (e - 1))
                                act.activation(h1[:, e % 2, 0, f - 1:f + 1, :], h1f[:, m // 2 % 2, :, :], ACT.Copy,
                                               scale=wsc[:, e, 1:2]).then_inc(c_hh, 1)
                        elif step[0] == "mm2" and step[3] == 1:
                            e, c = step[1:3]
                            n = SC[c][1]
                            act.wait_ge(m_2, 3 * e + c + 1)
                            if e == 0 and c == 0:
                                act.wait_ge(c_slot, 3)
                            if c == 0 and e >= 2:
                                act.wait_ge(d_scat, 48 * (e - 1))
                            act.activation(y[0:n, e % 2, c, :], pf[0:n, 2 + (3 * e + c) % 2, 0:D], ACT.Copy,
                                           scale=gs[0:n, e, c:c + 1]).then_inc(c_y, 1)
                        elif step[0] == "route":
                            act.wait_ge(c_soft, 2)
                            act.activation(lexp[:, :, :, :], ldif[:, :, :, :], ACT.Exp, scale=1.0 / XS)\
                                .then_inc(c_exp, 1)
                        elif step[0] == "hi":
                            n = step[1]
                            e = (n + 1) % NE
                            act.wait_ge(p_sc, 4 * n + 4)
                            if n >= 2:
                                act.wait_ge(p_out[e % 2], 32 * (n // 2))
                            for k in range(2):
                                last = act.activation(wr[:, e % 2, k, 0, :], raw[n % 2][:, k, :], ACT.Copy,
                                                      scale=wscale[:, k:k + 1])
                            last.then_inc(p_hi, 1)

                @block.vector
                def _(dve):
                    def normalise(src, stats, means, n, done, scale, out_, c_stats, c_means, c_scale):
                        for c in range(3):
                            last = dve.bn_stats(stats[:, c, :], src[:, c, :])
                        last.then_inc(c_stats, 1)
                        dve.wait_ge(c_stats, n)
                        for c in range(3):
                            last = dve.bn_aggr(means[:, c, :], stats[:, c, :])
                        last.then_inc(c_means, 1)
                        dve.wait_ge(c_means, n)
                        dve.wait_ge(c_scale, n)
                        for c in range(3):
                            last = dve.tensor_scalar(out_[:, c, :], src[:, c, :], means[:, c, 0:1], scale[:, c:c + 1],
                                                     ALU.subtract, ALU.mult)
                        last.then_inc(done, 1)

                    def score_mask(s, c, place):
                        n = CH[c][1]
                        src = pa[0:n, :, 256 * place:256 * (place + 1)].rearrange("p r (h n) -> p r h n", h=2)[:, :, :, 0:n]
                        dst = sc[0:n, c, :, 0:n].rearrange("p (h r) n -> p r h n", h=2)
                        m = mask[0:n, 0:n].unsqueeze(1).unsqueeze(1).broadcast_to([n, HPH, 2, n])
                        return dve.tensor_tensor(dst, src, m, ALU.mult)

                    def attention(s, p):
                        if p == 0:
                            dve.wait_ge(M_EMB, s + 1)
                            if s:
                                dve.wait_ge(d_h[s % 2], 16 * (s // 2 + s % 2))
                            dve.tensor_tensor(h[0:HP, s % 2, 0:2, :],
                                              pa[0:HP, 2, :].rearrange("p (c d) -> p c d", c=2), posb[0:HP, :, :],
                                              ALU.add).then_inc(c_h, 1)
                            dve.wait_ge(c_h, s + 1)
                            normalise(h[:, s % 2, :, :], st, mv, s + 1, c_xh, rs, xh, c_st, c_mv, c_rs)
                        elif p == 2:
                            dve.wait_ge(M_QK, s + 1)
                            dve.tensor_tensor(qT[:, :, :], pa[:, 0:2, 0:S], dq, ALU.mult).then_inc(c_q, 1)
                            dve.tensor_tensor(kT[:, :, :], pa[:, 2:4, 0:S], dk, ALU.mult).then_inc(c_k, 1)
                        elif p == 3:
                            dve.wait_ge(c_v, s + 1)
                            dve.tensor_tensor(
                                kt[0:HP, :, :].rearrange("p c (h e) -> p c h e", h=HEADS),
                                pa[0:HP, 0:2, D:2 * D].rearrange("p c (h e) -> p c h e", h=HEADS),
                                kd[0:HP, :, :].unsqueeze(3).broadcast_to([HP, 2, HEADS, HD]), ALU.mult)\
                                .then_inc(c_kt, 1)
                        elif p == 4:
                            dve.wait_ge(M_GS, s + 1)
                            dve.tensor_tensor(sbd[:, :, :, :].rearrange("p h u e -> p (h u) e"),
                                              pa[:, 0, :].rearrange("p (k e) -> p k e", k=4),
                                              bd.unsqueeze(1).broadcast_to([P, 4, P]), ALU.mult).then_inc(c_state, 1)
                            dve.wait_ge(c_th, s + 1)
                            dve.scalar_tensor_tensor(s2[:, :, :], th[:, :, :], 1.0, pa[:, 2:4, 0:S], ALU.add, ALU.mult)\
                                .then_inc(c_s2, 1)
                        elif p == 5:
                            dve.wait_ge(M_SA, s + 1)
                            score_mask(s, 0, 0)
                            score_mask(s, 1, 1).then_inc(c_scA, 1)
                        elif p == 6:
                            dve.wait_ge(M_SB, s + 1)
                            score_mask(s, 2, 0).then_inc(c_scB, 1)
                        elif p == 7:
                            dve.wait_ge(c_sq, s + 1)
                            dve.tensor_reduce(ss[:, :], sq[:, :, :].rearrange("p c (h e) -> p (c h) e", h=HEADS),
                                              AX.X, ALU.add).then_inc(c_ss, 1)
                            dve.wait_ge(c_rg, s + 1)
                            r = rg[:, :].rearrange("p (c h) -> p c h", c=3)
                            dve.tensor_tensor(
                                rn[0:HP, 0:2, :].rearrange("p c (h e) -> p (c h) e", h=HEADS),
                                pa[0:HP, 0, :].rearrange("p (k e) -> p k e", e=HD),
                                rg[0:HP, 0:2 * HEADS].unsqueeze(2).broadcast_to([HP, 2 * HEADS, HD]), ALU.mult)
                            dve.tensor_tensor(
                                rn[:, 2, :].rearrange("p (h e) -> p h e", h=HEADS),
                                pa[:, 1, 0:D].rearrange("p (h e) -> p h e", h=HEADS),
                                rg[:, 2 * HEADS:3 * HEADS].unsqueeze(2).broadcast_to([P, HEADS, HD]), ALU.mult)\
                                .then_inc(c_rn, 1)
                        elif p == 8:
                            dve.wait_ge(M_RT, s + 1)
                            dve.wait_ge(c_s2b, s + 1)
                            for hf in range(DH):
                                last = dve.scalar_tensor_tensor(oT[:, hf, :], pa[:, 2 + hf, 0:S], gn[:, 0, hf:hf + 1],
                                                                s2b[:, hf, :], ALU.mult, ALU.add)
                            last.then_inc(c_oT, 1)
                        elif p == 9:
                            dve.wait_ge(M_W2, s + 1)
                            if s >= 2:
                                dve.wait_ge(d_out[s % 2], 32 * (s // 2))
                            dve.tensor_tensor(h2[0:HP, s % 2, 0:2, :],
                                              pa[0:HP, 0, :].rearrange("p (c d) -> p c d", c=2),
                                              h[0:HP, s % 2, 0:2, :], ALU.add)
                            dve.tensor_tensor(h2[:, s % 2, 2, :], pa[:, 1, 0:D], h[:, s % 2, 2, :], ALU.add)\
                                .then_inc(c_h2, 1)
                            dve.wait_ge(c_h2, s + 1)
                            if s:
                                dve.wait_ge(c_hi, s)
                                dve.wait_ge(c_lo, s)
                            normalise(h2[:, s % 2, :, :], st2, mv2, s + 1, c_xs, rs2x, xs, c_st2, c_mv2, c_rs2x)
                        elif p == 11:
                            dve.wait_ge(M_RTR, s + 1)
                            dve.tensor_copy(lg[:, :, :, s], pa[:, 3, 0:3 * NE].rearrange("p (c e) -> p c e", c=3))\
                                .then_inc(c_lg, 1)

                    def softmax():
                        dve.wait_ge(c_lg, G)
                        over = lg[:, :, :, :].rearrange("p c e s -> p c s e")
                        dve.tensor_reduce(lmax[:, :, :], over, AX.X, ALU.max).then_inc(c_soft, 1)
                        dve.wait_ge(c_soft, 1)
                        dve.tensor_tensor(ldif[:, :, :, :], lg[:, :, :, :],
                                          lmax[:, :, :].unsqueeze(2).broadcast_to([P, 3, NE, G]), ALU.subtract)\
                            .then_inc(c_soft, 1)
                        dve.wait_ge(c_exp, 1)
                        dve.tensor_reduce(lsum[:, :, :], lexp[:, :, :, :].rearrange("p c e s -> p c s e"), AX.X, ALU.add)\
                            .then_inc(c_soft, 1)
                        dve.wait_ge(c_soft, 3)
                        dve.reciprocal(lrec[:, :, :], lsum[:, :, :]).then_inc(c_soft, 1)
                        dve.wait_ge(c_soft, 4)
                        dve.tensor_tensor(prob[:, :, :, :], lexp[:, :, :, :],
                                          lrec[:, :, :].unsqueeze(2).broadcast_to([P, 3, NE, G]), ALU.mult)\
                            .then_inc(c_prob, 1)

                    def choose(r):
                        if r < 0:
                            dve.wait_ge(m_pT, 1)
                            dve.tensor_copy(val[:, 0, 0:S], pa[0:ROWS, 1, 0:S]).then_inc(c_val, 1)
                            dve.wait_ge(c_val, 1)
                        else:
                            k = slice(8 * r, 8 * r + 8)
                            src, dst = val[:, 0 if r == 0 else 1, :], val[:, 1, :]
                            dve.max(top[:, k], src).then_inc(c_top, 1)
                            dve.wait_ge(c_top, 3 * r + 1)
                            dve.max_index(topi[:, k], top[:, k], src).then_inc(c_top, 1)
                            dve.match_replace(dst, top[:, k], src, -1.0).then_inc(c_top, 1)
                            dve.wait_ge(c_top, 3 * r + 3)

                    def chosen():
                        dve.tensor_copy(pack[:, :, 1], top[:, NSENT:]).then_inc(c_pick, 1)
                        dve.tensor_scalar(pack[:, :, 0].bitcast(U32), topi[:, NSENT:], rowbase, None, ALU.add)\
                            .then_inc(c_pick, 1)

                    def gathered(e, hf):
                        dve.wait_ge(m_g, DH * e + hf + 1)
                        dve.tensor_copy(xin[:, e % 2, hf, :, :], turned[:, hf, :, :]).then_inc(c_g, 1)

                    def split(e, f):
                        q = (FO * e + f) // 2
                        dve.wait_ge(c_hh, q + 1)
                        dve.scalar_tensor_tensor(h1[:, e % 2, 1, f - 1:f + 1, :], h1f[:, q % 2, :, :], wsc[:, e, 1:2],
                                                 h1[:, e % 2, 0, f - 1:f + 1, :], ALU.mult, ALU.subtract)\
                            .then_inc(c_hl, 1)

                    def prepare_reduce(n):
                        if n:
                            dve.wait_ge(p_amr, n)
                        dve.wait_ge(d_raw[n % 2], 32 * (n // 2 + 1))
                        dve.tensor_reduce(am[:, :], raw[n % 2], AX.X, ALU.max, apply_absolute_value=True)\
                            .then_inc(p_am, 1)

                    def prepare_scales(n):
                        e = (n + 1) % NE
                        dve.wait_ge(p_amr, n + 1)
                        if n:
                            dve.wait_ge(p_hi, n)
                        dve.tensor_scalar(amc[:, :], amr[:, :], 1e-18, None, ALU.max).then_inc(p_sc, 1)
                        dve.wait_ge(p_sc, 4 * n + 1)
                        dve.tensor_scalar(pw[:, :].bitcast(I32), amc[:, :].bitcast(I32), 0x7F800000, None,
                                          ALU.bitwise_and).then_inc(p_sc, 1)
                        dve.wait_ge(p_sc, 4 * n + 2)
                        dve.reciprocal(pinv[:, :], pw[:, :]).then_inc(p_sc, 1)
                        dve.wait_ge(p_sc, 4 * n + 3)
                        dve.tensor_scalar(wscale[:, :], pinv[:, :], 2.0 ** 14, None, ALU.mult)
                        dve.tensor_scalar(wsc[:, e, 0:1], pw[:, 0:1], 2.0 ** -14 / XS, None, ALU.mult)
                        dve.tensor_scalar(wsc[:, e, 1:2], pinv[:, 0:1], 2.0 ** 6, None, ALU.mult)
                        dve.scalar_tensor_tensor(wsc[:, e, 2:3], pw[:, 0:1], 2.0 ** -20, pw[:, 1:2], ALU.mult, ALU.mult)\
                            .then_inc(p_sc, 1)

                    def prepare_lo(n):
                        e = (n + 1) % NE
                        dve.wait_ge(p_sc, 4 * n + 4)
                        dve.wait_ge(p_hi, n + 1)
                        for k in range(2):
                            last = dve.scalar_tensor_tensor(wr[:, e % 2, k, 1, :], raw[n % 2][:, k, :],
                                                            wscale[:, k:k + 1], wr[:, e % 2, k, 0, :],
                                                            ALU.mult, ALU.subtract)
                        last.then_inc(p_lo, 1)

                    if experts:
                        dve.tensor_copy(slrow[:, :, :], slot[:, :, :, 0].bitcast(U32)).then_inc(c_slot, 1)
                        dve.tensor_scalar(slout[:, :, :], slot[:, :, :, 0].bitcast(U32), base[:, 0:1], None, ALU.add)\
                            .then_inc(c_slot, 1)
                        dve.tensor_tensor(gs[:, :, :], slot[:, :, :, 1],
                                          wsc[:, :, 2:3].broadcast_to([P, NE, 3]), ALU.mult).then_inc(c_slot, 1)
                        dve.wait_ge(c_slot, 2)
                        dve.tensor_scalar(base[:, :], base[:, :], float(G * S), None, ALU.add)
                    for step in steps:
                        if step[0] == "attn":
                            attention(*step[1:])
                        elif step[0] == "gather":
                            gathered(*step[1:])
                        elif step[0] == "mm1" and step[2] % 2:
                            split(*step[1:])
                        elif step[0] == "route":
                            softmax()
                        elif step[0] == "choose":
                            choose(step[1])
                        elif step[0] == "topk":
                            chosen()
                        elif step[0] == "reduce":
                            prepare_reduce(step[1])
                        elif step[0] == "scales":
                            prepare_scales(step[1])
                        elif step[0] == "lo":
                            prepare_lo(step[1])

                @block.gpsimd
                def _(pool):
                    def power(src, n, c_in, mid, c_mid, dst, c_out, width, mul):
                        pool.wait_ge(c_in, n)
                        pool.tensor_scalar(mid, src, mul, EPS, ALU.mult, ALU.add).then_inc(c_mid, 1)
                        pool.wait_ge(c_mid, n)
                        return pool.tensor_tensor(dst, mid, nhalf[:, 0:width], ALU.pow).then_inc(c_out, 1)

                    def attention(s, p):
                        if p == 0:
                            power(mv[:, :, 1], s + 1, c_mv, ve[:, :], c_ve, rs[:, :], c_rs, 3, 1.0)
                        elif p == 4:
                            pool.wait_ge(c_s2, s + 1)
                            for hf in range(DH):
                                last = pool.tensor_scalar(s2b[:, hf, :], s2[:, hf, :], gn[:, 1, hf:hf + 1], None, ALU.add)
                            last.then_inc(c_s2b, 1)
                        elif p == 7:
                            power(ss[:, :], s + 1, c_ss, ssb[:, :], c_ssb, rg[:, :], c_rg, 3 * HEADS, 1.0 / HD)
                        elif p == 9:
                            power(mv2[:, :, 1], s + 1, c_mv2, ve2[:, :], c_ve2, rs2[:, :], c_rs2, 3, 1.0)
                            pool.wait_ge(c_rs2, s + 1)
                            pool.tensor_scalar(rs2x[:, :], rs2[:, :], XS, 0.0, ALU.mult, ALU.add).then_inc(c_rs2x, 1)
                        elif p == 10:
                            pool.wait_ge(c_hi, s + 1)
                            pool.tensor_tensor(xhl[:, s % 2, :, 1, :], xs[:, :, :], xhl[:, s % 2, :, 0, :], ALU.subtract)\
                                .then_inc(c_lo, 1)

                    def fetch(e):
                        if e >= 2:
                            pool.wait_ge(m_g, DH * (e - 1))
                        for c, (k0, n) in enumerate(SC):
                            pool.indirect_dma_start(
                                out=xg[0:n, e % 2, c, :], out_offset=None, in_=scr_x[1 - parity],
                                in_offset=bass.IndirectOffsetOnAxis(ap=slrow[0:n, e, c:c + 1], axis=0))\
                                .then_inc(d_gath[e % 2], 16)

                    if experts:
                        pool.wait_ge(c_slot, 1)
                        fetch(0)
                        fetch(1)
                    for step in steps:
                        if step[0] == "attn":
                            attention(*step[1:])
                        elif step[0] == "gather" and step[2] == DH - 1 and step[1] + 2 < NE:
                            fetch(step[1] + 2)
                        elif step[0] == "mm2" and step[2:] == (2, 1):
                            e = step[1]
                            if e == 0:
                                pool.wait_ge(c_slot, 2)
                            pool.wait_ge(c_y, 3 * e + 3)
                            if e:
                                pool.wait_ge(d_scat, 48 * e)
                            for c, (k0, n) in enumerate(SC):
                                pool.indirect_dma_start(
                                    out=out_rows, out_offset=bass.IndirectOffsetOnAxis(ap=slout[0:n, e, c:c + 1], axis=0),
                                    in_=y[0:n, e % 2, c, :], in_offset=None, compute_op=ALU.add).then_inc(d_scat, 16)
                        elif step[0] == "reduce":
                            n = step[1]
                            pool.wait_ge(p_am, n + 1)
                            if n:
                                pool.wait_ge(p_sc, 4 * n)
                            pool.partition_all_reduce(amr[:, :], am[:, :], P, RADD_MAX).then_inc(p_amr, 1)
                    if attend:
                        pool.wait_ge(c_lo, G)
                    if experts:
                        pool.wait_ge(d_scat, 48 * NE)
                        for k in range(2):
                            pool.wait_ge(d_gath[k], 48 * (NE // 2))
                        pool.dma_reset(range(d_scat.num, d_gath[1].num + 1))
            barrier()

        body(0, 0, True, False, prepare=True)
        with nc.Fori(0, (NG - 2) // 2) as k:
            body(2 * k + 1, 1, True, True)
            body(2 * k + 2, 0, True, True)
        body(NG - 1, 1, True, True, ahead=False)
        body(NG, 0, False, True, more=False)


def constants():
    import numpy as np

    gamma = (1.0 - np.exp(np.linspace(np.log(1.0 / 512.0), np.log(1.0 / 32.0), HEADS))).astype(np.float32)
    gamma = gamma.astype(np.float64)
    t = np.zeros((P, C_ALL), np.float32)
    n, p = np.arange(S), np.arange(P)
    for hf in range(DH):
        per_row = gamma[HPH * hf + p // HD]
        t[:, C_DQ + S * hf:C_DQ + S * (hf + 1)] = per_row[:, None] ** n
        t[:, C_DK + S * hf:C_DK + S * (hf + 1)] = per_row[:, None] ** -n.astype(np.float64)
    for c in range(2):
        t[0:HP, C_KD + HEADS * c:C_KD + HEADS * (c + 1)] = gamma[None] ** -(HP * c + np.arange(HP, dtype=np.float64))[:, None]
    t[:, C_MASK:C_BD] = p[None] >= p[:, None]
    t[:, C_BD:C_ID] = p[None] // HD == p[:, None] // HD
    t[:, C_ID:C_ROW] = np.eye(P)
    t[0:ROWS, C_ROW] = S * (np.arange(ROWS) % G)
    return t


_INS = ["x", "txt", "L0_tok_W_embed", "L0_tok_b_embed", "L0_tok_pos_embed", "L0_attn_Wq", "L0_attn_Wk",
        "L0_attn_Wv", "L0_attn_W1", "L0_attn_W2", "L0_attn_gn_w", "L0_attn_gn_b", "L0_ffn_gate_w",
        "L0_ffn_w1", "L0_ffn_w2"]


def kernel(**inputs):
    import numpy as _np
    import concourse.bacc as _bacc
    from concourse import mybir as _mybir
    from concourse.bass_utils import run_bass_kernel_spmd as _run

    nc = _bacc.Bacc("TRN2", target_bir_lowering=False, num_devices=1)
    arrays, args = {}, []
    for name, a in [(n, inputs[n]) for n in _INS] + [("constants", constants())]:
        a = _np.ascontiguousarray(a)
        arrays[f"in_{name}_dram"] = a
        args.append(nc.dram_tensor(f"in_{name}_dram", a.shape, _mybir.dt.from_np(a.dtype), kind="ExternalInput").ap())
    args.append(nc.dram_tensor("out_dram", (B, S, D), F32, kind="ExternalOutput").ap())
    build(nc, *args)
    r = _run(nc, [arrays], core_ids=[0])
    return r.results[0]["out_dram"]
```

```python
from contextlib import ExitStack

import concourse.bass as bass
from concourse import mybir

F32 = mybir.dt.float32
F16 = mybir.dt.float16
U32 = mybir.dt.uint32
I32 = mybir.dt.int32
ALU = mybir.AluOpType
ACT = mybir.ActivationFunctionType
AX = mybir.AxisListType
RADD_MAX = bass.bass_isa.ReduceOp.max

P = 128
B = 32
SIDE, PATCH = 14, 16
CIN = 3
WPIX = SIDE * PATCH
NPATCH = SIDE * SIDE
NTXT = 128
S = NPATCH + NTXT
D = 256
DH = D // P
HEADS, HD = 8, 32
HPH = P // HD
HP = NPATCH // 2
CH = ((0, HP), (HP, HP), (NPATCH, NTXT))
NE, FF = 8, 1024
FO = FF // P
CAP = 2 * S // NE
PAD = CAP + 1
G = 4
NG = B // G
SL = G * CAP
SC = ((0, 128), (128, 128), (256, SL - 256))
ROWS = NE * G
ROUNDS = (CAP + 7) // 8
NSENT = ROUNDS * 8 - CAP
RW = S + NSENT
EPS = 1e-5
JH = PATCH // 2
CI = CIN * PATCH
ES = CIN * PATCH * PATCH // P
EX = 2 * CI
LEFT = ES
XS = 2048.0
WH = DH * FF
WP = 2 * WH
NA = 5
AQ, AV, AK, AW = range(4)
PASSES = ((0, 0), (1, 0), (0, 1))
DVE_PAIRS = (3,)
ACT_PAIRS = FO // 2 - len(DVE_PAIRS)
NPH = 12

C_DQ = 0
C_DK = C_DQ + DH * S
C_KD = C_DK + DH * S
C_MASK = C_KD + 2 * HEADS
C_BD = C_MASK + P
C_ID = C_BD + P
C_ROW = C_ID + P
C_ALL = C_ROW + 1


GAP = (0, 3, 3, 4, 3, 4, 4, 4, 11, 4, 0, 3)
GAP_LAST = 10
OVER = 2.5
GAP_ROUTE = 6
GAP_ROUND = 5
PREP_AT = ((0, ("reduce", 0)), (2, ("reduce", 1)), (2, ("scales",)), (3, ("hi", 0)), (4, ("hi", 1)),
           (4, ("lo", 0)), (5, ("lo", 1)), (6, ("reduce", 0)), (6, ("reduce", 1)), (7, ("scales",)),
           (7, ("hi", 0)), (7, ("hi", 1)), (7, ("lo", 0)), (10, ("lo", 1)))
COST = {"gather": 0.648, "mm1": 6 * 0.324, "mm2": 12 * 0.324, "back": 1.3}


def expert_steps():
    def begin(e):
        return ([("mm1", e, 0), ("mm1", e, 1)] if e < NE else []) + \
            ([("gather", e + 1, hf) for hf in range(DH)] if e + 1 < NE else [])

    steps = [("gather", 0, hf) for hf in range(DH)] + begin(0)
    for e in range(NE):
        steps += [("mm1", e, 2), ("mm1", e, 3)] + ([("back", e - 1)] if e else [])
        steps += [("mm1", e, f) for f in range(4, FO)] + begin(e + 1)
        steps += [("mm2", e, dh, half) for half in range(2) for dh in range(DH)]
    return steps + [("back", NE - 1)]


def plan(attend, experts, prepare):
    front = []
    if attend:
        between = {6: 0, 7: 1, 8: 2, 9: 3} if prepare else {9: 0}
        front = [(GAP[0], ("attn", 0, 0))]
        for s in range(G):
            for p in range(1, NPH):
                if s == 0 or p not in between.values():
                    front.append((GAP_LAST if (s, p) == (G - 1, 10) else GAP[p], ("attn", s, p)))
                if p in between and s + 1 < G:
                    front.append((0, ("attn", s + 1, between[p])))
        front += [(GAP_ROUTE, ("route",)), (0, ("choose", -1))]
        front += [(GAP_ROUND, ("choose", r)) for r in range(ROUNDS)] + [(0, ("topk",))]
    back = []
    if experts:
        back = expert_steps()
    if prepare:
        where = {}
        for n in range(NE):
            half = len(PREP_AT) // 2
            for p, (kind, *k) in PREP_AT[half * (n % 2):half * (n % 2 + 1)]:
                where.setdefault(front[NPH * (n // 2) + p][1], []).append((kind, n, *k))
    steps = []
    for gap, step in front:
        if prepare and step[0] == "attn":
            steps += where.get(step, [])
        while experts and back and gap > 0:
            gap -= COST[back[0][0]]
            if gap < -OVER:
                break
            steps.append(back.pop(0))
        steps.append(step)
    return steps + back


def build(nc, x, txt, We, be, pos, Wq, Wk, Wv, W1, W2, gnw, gnb, gate, w1, w2, const, out):
    ctx = ExitStack()
    with ctx:
        def sb(name, shape, dt=F32):
            return ctx.enter_context(nc.sbuf_tensor(name, shape, dt))

        sems = []

        def sem(name):
            h = ctx.enter_context(nc.semaphore(name))
            sems.append(h)
            return h

        wscr = nc.dram_tensor("w_split", (NE, 2, P, WP), F16, kind="Internal").ap()
        scr_x = [nc.dram_tensor(f"x_split{k}", (G * S, 2 * D), F16, kind="Internal").ap() for k in range(2)]
        scr_slot = nc.dram_tensor("choice_slot", (ROWS * CAP, 2), F32, kind="Internal").ap()
        out_rows = out.rearrange("b s d -> (b s) d")

        cst = sb("cst", [P, C_ALL])
        dq = cst[:, C_DQ:C_DK].rearrange("p (h s) -> p h s", h=DH)
        dk = cst[:, C_DK:C_KD].rearrange("p (h s) -> p h s", h=DH)
        kd = cst[:, C_KD:C_MASK].rearrange("p (c h) -> p c h", c=2)
        mask = cst[:, C_MASK:C_BD]
        bd = cst[:, C_BD:C_ID]
        ident = cst[:, C_ID:C_ROW]
        rowbase = cst[0:ROWS, C_ROW:C_ALL]
        ident16 = sb("ident16", [P, P], F16)
        we = sb("we", [P, ES, D])
        posb = sb("posb", [P, 2, D])
        bebc = sb("bebc", [P, D])
        aw = sb("aw", [P, 2, NA, DH, P], F16)
        vsum = sb("vsum", [P, DH])
        w2g = sb("w2g", [P, DH, D])
        undo = sb("undo", [P, 5])
        gn = sb("gn", [P, 2, DH])
        gateT = sb("gateT", [P, DH, NE])
        unq, unv, unk, unw, unth = (undo[:, k:k + 1] for k in range(5))
        nhalf = sb("nhalf", [P, 3 * HEADS])
        wsc = sb("wsc", [P, NE, 3])

        xt = sb("xt", [P, SIDE, WPIX])
        xe = sb("xe", [P, SIDE, WPIX])
        h = sb("h", [P, 2, 3, D])
        h2 = sb("h2", [P, 2, 3, D])
        st = sb("st", [P, 3, 6])
        mv = sb("mv", [P, 3, 2])
        ve = sb("ve", [P, 3])
        rs = sb("rs", [P, 3])
        xh = sb("xh", [P, 3, D])
        x2T = sb("x2T", [P, DH, 3 * P])
        xT_loop = x2T[:, :, :].rearrange("p h n -> p (h n)").bitcast(F16)[:, 0:2 * DH * S]\
            .rearrange("p (k h n) -> p k h n", k=2, h=DH)
        qT = sb("qT", [P, DH, S])
        kT = sb("kT", [P, DH, S])
        kt = sb("kt", [P, 2, D])
        v = sb("v", [P, 3, D])
        s2 = sb("s2", [P, DH, S])
        s2b = s2
        sbd = sb("sbd", [P, DH, 2, P])
        sc = sb("sc", [P, 3, HEADS, P])
        sq = sb("sq", [P, 3, D])
        ss = sb("ss", [P, 3 * HEADS])
        ssb = sb("ssb", [P, 3 * HEADS])
        rg = sb("rg", [P, 3 * HEADS])
        rn = xh
        oT = sb("oT", [P, DH, S])
        th = oT
        st2 = sb("st2", [P, 3, 6])
        mv2 = sb("mv2", [P, 3, 2])
        ve2 = sb("ve2", [P, 3])
        rs2 = sb("rs2", [P, 3])
        rs2x = sb("rs2x", [P, 3])
        xs = sb("xs", [P, 3, D])
        lg = sb("lg", [P, 3, NE, G])
        lmax = sb("lmax", [P, 3, G])
        ldif = sb("ldif", [P, 3, NE, G])
        lexp = sb("lexp", [P, 3, NE, G])
        lsum = sb("lsum", [P, 3, G])
        lrec = sb("lrec", [P, 3, G])
        prob = sb("prob", [P, 3, NE, G])
        val = sb("val", [ROWS, 2, RW])
        top = sb("top", [ROWS, ROUNDS * 8])
        topi = sb("topi", [ROWS, ROUNDS * 8], U32)
        pack = sb("pack", [ROWS, CAP, 2])

        xhl = sb("xhl", [P, 2, 3, 2, D], F16)

        idx = sb("idx", [CAP, ROWS], U32)

        slot = sb("slot", [P, NE, 3, 2])
        slout = sb("slout", [P, NE, 3], U32)
        base = sb("base", [P, 1])
        gs = sb("gs", [P, NE, 3])
        n_y, n_xg, n_xin = 2 * 3 * D, G * 2 * D, 2 * DH * SL
        ring = sb("ring", [P, n_y + n_xg + n_xin])
        y = ring[:, 0:n_y].rearrange("p (b c d) -> p b c d", b=2, c=3)
        xg = ring[:, n_y:n_y + n_xg].bitcast(F16).rearrange("p (b s d) -> p b s d", b=2, s=G)
        xin = ring[:, n_y + n_xg:].bitcast(F16).rearrange("p (b h k n) -> p b h k n", b=2, h=DH, k=2)
        wr = sb("wr", [P, 2, 2, 2, WH], F16)
        yT = sb("yT", [P, DH, SL])
        h1f = sb("h1f", [P, 2, 2, SL])
        h1 = sb("h1", [P, 2, 2, FO, SL], F16)

        raw = [t.rearrange("p (k w) -> p k w", k=2) for t in
               (ring[:, 0:WP], h1[:, :, :, :, :].rearrange("p a b c d -> p (a b c d)").bitcast(F32)[:, 0:WP])]
        aw32 = h1f[:, :, :, :].rearrange("p a b n -> p (a b n)")[:, 0:NA * D]\
            .rearrange("p (k h n) -> p k h n", k=NA, h=DH)
        xh_ahead = h1f[:, :, :, :].rearrange("p a b n -> p (a b n)")[:, 0:3 * D].rearrange("p (c d) -> p c d", c=3)
        xT_ahead = yT[:, :, :].rearrange("p h n -> p (h n)").bitcast(F16)\
            .rearrange("p (k h n) -> p k h n", k=2, h=DH)
        aam, aamr, apw, apinv, ascale = (sb("attn_" + n, [P, 4]) for n in ("am", "amr", "pw", "pinv", "scale"))
        am = sb("am", [P, 2])
        amr = sb("amr", [P, 2])
        amc = sb("amc", [P, 2])
        pw = sb("pw", [P, 2])
        pinv = sb("pinv", [P, 2])
        wscale = sb("wscale", [P, 2])

        pa = ctx.enter_context(nc.psum_tensor("pa", [P, 4, 512], F32))
        pf = ctx.enter_context(nc.psum_tensor("pf", [P, 4, 512], F32))
        turned = pf[:, 0:2, 0:G * PAD].bitcast(F16).rearrange("p b (k s n) -> p b k s n", k=2, s=G)

        def taken(e, hf):
            return xin[:, e % 2, hf, :, :].rearrange("p k (s n) -> p k s n", s=G)

        d_x, d_h = sem("d_x"), [sem("d_txt0"), sem("d_txt1")]
        d_w = [[sem(f"d_w{k + 1}_{e}") for e in ("even", "odd")] for k in range(2)]
        d_raw = [sem("d_raw0"), sem("d_raw1")]
        d_out = [sem("d_out0"), sem("d_out1")]
        d_c2, d_tail = sem("d_slot_out"), sem("d_slot_in")
        d_xh = [sem("d_xh0"), sem("d_xh1")]
        d_scat, d_gath = sem("d_scatter"), [sem("d_gather0"), sem("d_gather1")]
        d_setup, d_weights, c_ready, c_xe = sem("d_setup"), sem("d_weights"), sem("c_ready"), sem("c_xe")
        c_aam, c_aamr, c_awhi = sem("c_attn_am"), sem("c_attn_amr"), sem("c_attn_hi")
        names = ("embed", "xT", "qk", "vk", "gated_state", "scoresA", "scoresB", "ret", "retT", "w2", "x2T", "router")
        mm = [sem("mm_" + n) for n in names]
        (M_EMB, M_XT, M_QK, M_VK, M_GS, M_SA, M_SB, M_RET, M_RT, M_W2, M_X2T, M_RTR) = mm
        c_h, c_st, c_mv, c_ve, c_rs, c_xh = (sem("c_" + n) for n in ("h", "st", "mv", "ve", "rs", "xh"))
        c_xThi, c_xT, c_q, c_k, c_v, c_kt, c_th, c_s2, c_s2b, c_state = (
            sem("c_" + n) for n in ("xT_hi", "xT", "q", "k", "v", "kt", "th", "s2", "s2b", "state"))
        c_scA, c_scB, c_sq, c_ss, c_ssb, c_rg, c_rn, c_oT, c_h2 = (
            sem("c_" + n) for n in ("scA", "scB", "sq", "ss", "ssb", "rg", "rn", "oT", "h2"))
        c_st2, c_mv2, c_ve2, c_rs2, c_rs2x, c_xs, c_hi, c_lo, c_x2T, c_lg = (
            sem("c_" + n) for n in ("st2", "mv2", "ve2", "rs2", "rs2x", "xs", "hi", "lo", "x2T", "lg"))
        c_soft, c_exp, c_prob, m_pT, c_val, c_top, c_pick, m_iT = (
            sem("c_" + n) for n in ("soft", "exp", "prob", "pT", "val", "top", "pick", "iT"))
        m_g, c_g, c_slot = sem("mm_gather"), sem("c_gather"), sem("c_slot")
        m_1, m_2, m_b, c_gelu, c_hh, c_hd, c_hl, c_yT, c_y = (
            sem(n) for n in ("mm_1", "mm_2", "mm_back", "c_gelu", "c_hi_act", "c_hi_dve", "c_hl", "c_yT", "c_y"))
        p_am, p_amr, p_sc, p_lo = (sem("p_" + n) for n in ("am", "amr", "sc", "lo"))
        p_hi = [sem("p_hi_act"), sem("p_hi_pool")]
        p_out = [sem("p_out0"), sem("p_out1")]
        s_v, s_pool = sem("s_v"), sem("s_pool")

        def barrier():
            nc.sync.sem_clear(range(sems[0].num, sems[-1].num + 1))
            nc.all_engine_barrier(sem_only=True)

        def patches(t, j, c):
            rows = SIDE // 2
            return t[:, rows * c:rows * (c + 1), :].rearrange("p a (b j) -> p a b j", j=PATCH)[:, :, :, j]

        def load_image(sp, i, s):
            def rows(c, shift):
                return x[i, c].rearrange("(a i) w -> i a w", i=PATCH)[:, :, shift:WPIX]
            for half in range(2):
                for c in range(CIN):
                    q = CI * half + PATCH * c
                    sp.dma_start(xt[q:q + PATCH, :, 0:WPIX - JH * half], rows(c, JH * half)).then_inc(d_x, 16)
                q = EX + PATCH * half
                sp.dma_start(xt[q:q + PATCH, :, :], rows(half, 0)).then_inc(d_x, 16)
                sp.dma_start(xe[q:q + PATCH, :, 0:WPIX - JH * half], rows(2, JH * half)).then_inc(d_x, 16)
            sp.dma_start(h[:, s % 2, 2, :], txt[i]).then_inc(d_h[s % 2], 16)
        n_x = 16 * 2 * (CIN + 2)

        def take_left(act):
            def col(t, j):
                return t[EX:P, :, :].rearrange("p a (b j) -> p a b j", j=PATCH)[:, :, :, j:j + 2]
            act.copy(col(xt, 0), col(xt, LEFT))
            act.copy(col(xt, 2), col(xt, JH + LEFT))
            act.copy(col(xt, 4), col(xe, LEFT)).then_inc(c_xe, 1)

        with nc.Block(no_gpsimd_drain=True) as block:
            @block.sync
            def _(sp):
                sp.dma_start(posb[0:HP, :, :], pos[0].rearrange("(c p) d -> p c d", c=2)).then_inc(d_setup, 16)
                sp.dma_start(bebc[:, :], be.partition_broadcast(P)).then_inc(d_setup, 16)
                rows = We.rearrange("(k j) e -> k j e", j=PATCH)
                two = slice(2 * PATCH, 3 * PATCH)
                for half in range(2):
                    j, q = JH * half, EX + PATCH * half
                    sp.dma_start(we[CI * half:CI * (half + 1), :, :], rows[:, j:j + ES, :]).then_inc(d_setup, 16)
                    sp.dma_start(we[EX:P, 2 * half:2 * half + 2, :], rows[0:P - EX, j + LEFT:j + JH, :])\
                        .then_inc(d_setup, 16)
                    sp.dma_start(we[q:q + PATCH, 4:6, :], rows[two, j + LEFT:j + JH, :]).then_inc(d_setup, 16)
                load_image(sp, 0, 0)
                sp.dma_start(cst[:, :], const).then_inc(d_setup, 16)
                sp.wait_ge(d_x, n_x)
                sp.wait_ge(d_h[0], 16)
            n_setup = 16 * (3 + 6)

            @block.scalar
            def _(act):
                act.wait_ge(d_x, n_x)
                take_left(act)

            @block.gpsimd
            def _(pool):
                pool.memset(slot[:, :, :, :], 0.0).then_inc(s_pool, 1)
                pool.wait_ge(s_pool, 1)

            @block.vector
            def _(dve):
                dve.memset(aw32[:, AQ:AK + 1, :, :], 0.0)
                dve.memset(h[:, :, 0:2, :], 0.0)
                dve.memset(h2[:, :, :, :], 0.0)
                dve.memset(sq[:, :, :], 0.0)
                dve.memset(nhalf[:, :], -0.5)
                dve.memset(base[:, :], 0.0)
                for k in range(NSENT):
                    dve.memset(val[:, 0, S + k:S + k + 1], 2.0 + k)
                dve.wait_ge(d_setup, n_setup)
                dve.tensor_copy(ident16[:, :], ident)
                dve.tensor_tensor(posb[0:HP, :, :], posb[0:HP, :, :],
                                  bebc[0:HP, :].unsqueeze(1).broadcast_to([HP, 2, D]), ALU.add)
        barrier()

        def body(g, parity, attend, experts, prepare=False, more=True, ahead=True):
            steps = plan(attend, experts, prepare)
            pp, (p_emb, b_emb) = (pf, (pf, 3)) if prepare else (pa, (pa, 2))
            xT = xT_ahead if prepare else xT_loop

            def xh_of(s):
                return xh_ahead if prepare and s else xh

            def img(s):
                return g * G + s

            with nc.Block(no_gpsimd_drain=True) as block:
                @block.sync
                def _(sp):
                    def load_raw(n, k):
                        e = (n + 1) % NE
                        src = (w1[e].rearrange("(h p) f -> p h f", h=DH), w2[e].rearrange("(o p) d -> p o d", o=FO))[k]
                        sp.dma_start(raw[n % 2][:, k, :].rearrange("p (a b) -> p a b", a=src.shape[1]), src)\
                            .then_inc(d_raw[n % 2], 16)

                    if prepare:
                        for n in range(2):
                            for k in range(2):
                                load_raw(n, k)
                    if experts:
                        sp.dma_start(scr_slot.rearrange("(r k) t -> r (k t)", r=ROWS),
                                     pack[:, :, :].rearrange("r k t -> r (k t)")).then_inc(d_c2, 16)
                        sp.wait_ge(d_c2, 16)
                        per = scr_slot.rearrange("(e k) t -> e k t", e=NE)
                        with nc.allow_non_contiguous_dma(reason="two words per slot"):
                            for c, (k0, n) in enumerate(SC):
                                sp.dma_start(slot[0:n, :, c, :], per[:, k0:k0 + n, :].rearrange("e k t -> k e t"))\
                                    .then_inc(d_tail, 16)
                    for step in steps:
                        if step[0] == "attn" and step[2] == 0 and (ahead or step[1] + 1 < G):
                            s = step[1] + 1
                            sp.wait_ge(M_EMB, s)
                            if s >= 2:
                                sp.wait_ge(c_h2, s - 1)
                            load_image(sp, img(s), s)
                        if step[0] == "attn" and step[2] == 10:
                            s = step[1]
                            sp.wait_ge(c_hi, s + 1)
                            sp.wait_ge(c_lo, s + 1)
                            rows = scr_x[parity].rearrange("(g s) d -> g s d", g=G)[s]
                            sp.dma_start(rows[0:NPATCH].rearrange("(c p) d -> p c d", c=2),
                                         xhl[0:HP, s % 2, 0:2, :, :].rearrange("p c k d -> p c (k d)"))\
                                .then_inc(d_xh[s % 2], 16)
                            sp.dma_start(rows[NPATCH:S],
                                         xhl[:, s % 2, 2, :, :].rearrange("p k d -> p (k d)")).then_inc(d_xh[s % 2], 16)
                        if step[0] == "attn" and step[2] == 9:
                            s = step[1]
                            sp.wait_ge(c_h2, s + 1)
                            rows = out[img(s)]
                            sp.dma_start(rows[0:NPATCH].rearrange("(c p) d -> p c d", c=2), h2[0:HP, s % 2, 0:2, :])\
                                .then_inc(d_out[s % 2], 16)
                            sp.dma_start(rows[NPATCH:S], h2[:, s % 2, 2, :]).then_inc(d_out[s % 2], 16)
                        if step[0] == "lo":
                            n, k = step[1:]
                            e = (n + 1) % NE
                            sp.wait_ge(p_hi[k], n + 1)
                            sp.wait_ge(p_lo, 2 * n + k + 1)
                            if n + 2 < NE:
                                load_raw(n + 2, k)
                            sp.dma_start(wscr[e, k], wr[:, e % 2, k, :, :].rearrange("p a b -> p (a b)"))\
                                .then_inc(p_out[e % 2], 16)
                    if prepare:
                        for k in range(2):
                            sp.wait_ge(p_out[k], 32 * (NE // 2))
                    if attend:
                        for k in range(2):
                            sp.wait_ge(d_out[k], 32 * (G // 2))
                            sp.wait_ge(d_xh[k], 32 * (G // 2))
                    if attend and ahead:
                        sp.wait_ge(d_x, n_x * G)
                        sp.wait_ge(d_h[0], 16 * (G // 2))
                    if experts and more:
                        for k in range(2):
                            sp.wait_ge(d_w[k][0], 16 * (NE // 2))

                @block.tensor
                def _(pe):
                    def embed(s):
                        if s:
                            pe.wait_ge(d_x, n_x * s)
                            pe.wait_ge(c_xe, s)
                            if prepare:
                                pe.wait_ge(c_k, s)
                            else:
                                pe.wait_ge(c_oT, s)
                        for c in range(2):
                            for j in range(ES):
                                last = pe.matmul(p_emb[0:HP, b_emb, D * c:D * (c + 1)], patches(xt, j, c), we[:, j, :],
                                                 start=j == 0, stop=j == ES - 1)
                        last.then_inc(M_EMB, 1)

                    def turn(src, dst, bank, pad, chunks=(0, 1, 2)):
                        for hf in range(DH):
                            for c in chunks:
                                t0, n = (P * c, P) if pad else CH[c]
                                last = pe.transpose(dst[:, bank + hf, t0:t0 + n], src[0:n, c, P * hf:P * (hf + 1)],
                                                    ident[0:n, 0:n])
                        return last

                    def project_qk(s):
                        pe.wait_ge(c_xT, s + 1)
                        if prepare and s == 0:
                            pe.wait_ge(c_ready, 1)
                        if s and not prepare:
                            pe.wait_ge(c_lg, s)
                        for k in range(2):
                            for hf in range(DH):
                                for n, (wp, xp) in enumerate(PASSES):
                                    last = pe.matmul(pp[:, 2 * k + hf, 0:S], aw[:, wp, (AQ, AK)[k], hf, :],
                                                     xT[:, xp, hf, :], start=n == 0, stop=n == 2)
                        last.then_inc(M_QK, 1)

                    def project_vk(s):
                        pe.wait_ge(c_q, s + 1)
                        for c, (t0, n) in enumerate(CH):
                            if c == 2:
                                pe.wait_ge(c_k, s + 1)
                            w = 2 if c < 2 else 1
                            bank = pp[0:n, c, :].rearrange("p (w h e) -> p w h e", w=2, h=DH)
                            for hf in range(DH):
                                for k, (wp, xp) in enumerate(PASSES):
                                    last = pe.matmul(bank[:, 0:w, hf, :], xT[:, xp, hf, t0:t0 + n],
                                                     aw[:, wp, AV:AV + w, hf, :], start=hf == 0 and k == 0,
                                                     stop=k == 2, skip_group_check=True)
                        last.then_inc(M_VK, 1)

                    def gated_state(s):
                        if s and prepare:
                            pe.wait_ge(c_lg, s)
                        for m in (1, 0):
                            if m == 0:
                                pe.wait_ge(c_v, s + 1)
                            for hf in range(DH):
                                for k, (wp, xp) in enumerate(PASSES):
                                    pe.matmul(pa[:, 2 + m, 0:S], aw[:, wp, AW + m, hf, :], xT[:, xp, hf, :],
                                              start=hf == 0 and k == 0, stop=hf == DH - 1 and k == 2)
                        pe.wait_ge(c_kt, s + 1)
                        for hf in range(DH):
                            for c in range(2):
                                o = P * (2 * hf + c)
                                last = pe.matmul(pa[:, 0, o:o + P], kt[0:HP, c, P * hf:P * (hf + 1)],
                                                 v[0:HP, c, P * hf:P * (hf + 1)], start=True, stop=True)
                        last.then_inc(M_GS, 1)

                    def scores(c, place):
                        t0, n = CH[c]
                        for head in range(HEADS):
                            hf, r = head // HPH, head % HPH
                            a = slice(HD * r, HD * (r + 1))
                            o = 256 * place + P * hf
                            last = pe.matmul(pa[0:n, r, o:o + n], kT[a, hf, t0:t0 + n], qT[a, hf, t0:t0 + n],
                                             start=True, stop=True)
                        return last

                    def retain(s):
                        pe.wait_ge(c_state, 2 * s + 2)
                        pe.wait_ge(c_scB, s + 1)
                        for c, (t0, n) in enumerate(CH):
                            bank, o = (0, D * c) if c < 2 else (1, 0)
                            if c:
                                for hf in range(DH):
                                    pe.matmul(pa[0:n, bank, o + P * hf:o + P * (hf + 1)], qT[:, hf, t0:t0 + n],
                                              sbd[:, hf, c - 1, :], start=hf == 0, stop=False, skip_group_check=True)
                            for head in range(HEADS):
                                a = slice(HD * head, HD * (head + 1))
                                last = pe.matmul(pa[0:n, bank, o + HD * head:o + HD * (head + 1)],
                                                 sc[0:n, c, head, 0:n], v[0:n, c, a],
                                                 start=c == 0 and head == 0, stop=True, skip_group_check=True)
                            if c:
                                last.then_inc(M_RET, 1)

                    def mix(s):
                        pe.wait_ge(c_oT, s + 1)
                        for c, (t0, n) in enumerate(CH):
                            o, bank = (D * c, 0) if c < 2 else (0, 1)
                            for hf in range(DH):
                                last = pe.matmul(pa[0:n, bank, o:o + D], oT[:, hf, t0:t0 + n], w2g[:, hf, :],
                                                 start=hf == 0, stop=hf == DH - 1)
                        last.then_inc(M_W2, 1)

                    def attention(s, p):
                        if p == 0:
                            embed(s)
                        elif p == 1:
                            pe.wait_ge(c_xh, s + 1)
                            turn(xh_of(s), pp, 1, False).then_inc(M_XT, 1)
                        elif p == 2:
                            project_qk(s)
                        elif p == 3:
                            project_vk(s)
                        elif p == 4:
                            gated_state(s)
                        elif p == 5:
                            pe.wait_ge(c_s2, s + 1)
                            pe.wait_ge(c_state, 2 * s + 1)
                            scores(0, 0)
                            scores(1, 1).then_inc(M_SA, 1)
                        elif p == 6:
                            pe.wait_ge(c_scA, s + 1)
                            scores(2, 0).then_inc(M_SB, 1)
                        elif p == 7:
                            retain(s)
                        elif p == 8:
                            pe.wait_ge(c_rn, 2 * s + 1)
                            turn(rn, pa, 2, False, (0, 1))
                            pe.wait_ge(c_rn, 2 * s + 2)
                            turn(rn, pa, 2, False, (2,)).then_inc(M_RT, 1)
                        elif p == 9:
                            mix(s)
                        elif p == 10:
                            pe.wait_ge(c_xs, s + 1)
                            turn(xs, pa, 0, True).then_inc(M_X2T, 1)
                        elif p == 11:
                            pe.wait_ge(c_x2T, s + 1)
                            for c in range(3):
                                for hf in range(DH):
                                    last = pe.matmul(pa[:, 3, NE * c:NE * (c + 1)], x2T[:, hf, P * c:P * (c + 1)],
                                                     gateT[:, hf, :], start=hf == 0, stop=hf == DH - 1)
                            last.then_inc(M_RTR, 1)

                    def gather(e, hf):
                        if hf == 0:
                            pe.wait_ge(d_gath[e % 2], 16 * G * (e // 2 + 1))
                        if e:
                            pe.wait_ge(c_gelu, FO * (e - 1) + hf + 1)
                        for part in range(2):
                            for s in range(G):
                                o = D * part + P * hf
                                last = pe.transpose(turned[:, hf, part, s, 0:CAP], xg[0:CAP, e % 2, s, o:o + P],
                                                    ident16[0:CAP, 0:CAP])
                        last.then_inc(m_g, 1)

                    def first(e, f):
                        m = FO * e + f
                        if f == 0:
                            pe.wait_ge(c_g, DH * (e + 1))
                        if f in (2, 3) and e < NE - 1:
                            pe.wait_ge(c_g, DH * (e + 1) + f - 1)
                        if f == 0 and e:
                            pe.wait_ge(d_w[0][e % 2], 16 * ((e + 1) // 2))
                        if m >= 2:
                            pe.wait_ge(c_gelu, m - 1)
                        k = 0
                        for hf in range(DH):
                            for wp, xp in ((0, 0), (1, 0), (0, 1)):
                                o = FF * hf + P * f
                                last = pe.matmul(pf[:, m % 2, 0:SL], wr[:, e % 2, 0, wp, o:o + P], xin[:, e % 2, hf, xp, :],
                                                 start=k == 0, stop=k == 5)
                                k += 1
                        last.then_inc(m_1, 1)

                    def second(e, dh, half):
                        if dh == 0 and half == 0:
                            if e:
                                pe.wait_ge(d_w[1][e % 2], 16 * ((e + 1) // 2))
                                pe.wait_ge(c_y, 3 * e)
                            pe.wait_ge(c_hl, 4 * e + 2)
                        if dh == 0 and half == 1:
                            pe.wait_ge(c_hl, 4 * e + 4)
                        k = 3 * FO // 2 * half
                        for f in range(FO // 2 * half, FO // 2 * (half + 1)):
                            for wp, hp in PASSES:
                                o = D * f + P * dh
                                last = pe.matmul(pf[:, 2 + dh, 0:SL], wr[:, e % 2, 1, wp, o:o + P],
                                                 h1[:, e % 2, hp, f, :], start=k == 0, stop=k == 3 * FO - 1)
                                k += 1
                        if half:
                            last.then_inc(m_2, 1)

                    def turn_back(e):
                        pe.wait_ge(c_yT, e + 1)
                        for c, (k0, n) in enumerate(SC):
                            bank, o = (2, D * c) if c < 2 else (3, 0)
                            for dh in range(DH):
                                last = pe.transpose(pf[0:n, bank, o + P * dh:o + P * (dh + 1)], yT[:, dh, k0:k0 + n],
                                                    ident)
                        last.then_inc(m_b, 1)

                    for step in steps:
                        if step[0] == "attn":
                            attention(*step[1:])
                        elif step[0] == "gather":
                            gather(*step[1:])
                        elif step[0] == "mm1":
                            first(*step[1:])
                        elif step[0] == "back":
                            turn_back(step[1])
                        elif step[0] == "mm2":
                            second(*step[1:])
                        elif step[0] == "route":
                            pe.wait_ge(c_prob, 1)
                            for c, (t0, n) in enumerate(CH):
                                last = pe.transpose(pa[0:ROWS, 1, t0:t0 + n],
                                                    prob[0:n, c, :, :].rearrange("p e s -> p (e s)"), ident[0:n, 0:n])
                            last.then_inc(m_pT, 1)

                    if attend:
                        pe.wait_ge(c_pick, 1)
                        pe.transpose(pa[0:CAP, 0, 0:ROWS], pack[:, :, 0], ident[0:ROWS, 0:ROWS]).then_inc(m_iT, 1)

                @block.scalar
                def _(act):
                    def load_weights(e, k):
                        if e >= NE and not more:
                            return
                        e = e % NE
                        act.dma_start(wr[:, e % 2, k, :, :].rearrange("p a b -> p (a b)"), wscr[e, k])\
                            .then_inc(d_w[k][e % 2], 16)

                    def attention(s, p):
                        if p == 1:
                            act.wait_ge(M_XT, s + 1)
                            act.activation(xT[:, 0, :, :], pp[:, 1:3, 0:S], ACT.Copy, scale=XS).then_inc(c_xThi, 1)
                        elif p == 3:
                            act.wait_ge(M_VK, s + 1)
                            act.activation(v[0:HP, 0:2, :], pp[0:HP, 0:2, 0:D], ACT.Copy, scale=undo[0:HP, AV:AV + 1])
                            act.activation(v[:, 2, :], pp[:, 2, 0:D], ACT.Copy, scale=unv).then_inc(c_v, 1)
                        elif p == 4:
                            act.wait_ge(M_GS, s + 1)
                            act.activation(th[:, :, :], pa[:, 2:4, 0:S], ACT.Tanh, scale=unth).then_inc(c_th, 1)
                        elif p == 5 and (ahead or s + 1 < G):
                            act.wait_ge(d_x, n_x * (s + 1))
                            take_left(act)
                        elif p == 7:
                            act.wait_ge(M_RET, 2 * s + 1)
                            act.square(sq[0:HP, 0:2, :], pa[0:HP, 0, :].rearrange("p (c d) -> p c d", c=2)).then_inc(c_sq, 1)
                            act.wait_ge(M_RET, 2 * s + 2)
                            act.square(sq[:, 2, :], pa[:, 1, 0:D]).then_inc(c_sq, 1)
                        elif p == 10:
                            act.wait_ge(c_xs, s + 1)
                            if s >= 2:
                                act.wait_ge(d_xh[s % 2], 32 * (s // 2))
                            act.copy(xhl[:, s % 2, :, 0, :], xs[:, :, :]).then_inc(c_hi, 1)
                            act.wait_ge(M_X2T, s + 1)
                            act.copy(x2T[:, :, :], pa[:, 0:2, 0:3 * P]).then_inc(c_x2T, 1)

                    if prepare:
                        for r in range(HPH):
                            a = slice(HD * r, HD * (r + 1))
                            for k, w in ((AV, Wv), (AQ, Wq), (AK, Wk)):
                                act.dma_start(aw32[a, k, :, a], w.rearrange("(h r) d e -> r d h e", h=DH)[r]).then_inc(d_weights, 16)
                        for m in range(DH):
                            act.dma_start(aw32[:, AW + m, :, :], W1.rearrange("(h p) d -> p h d", h=DH)[:, :, P * m:P * (m + 1)])\
                                .then_inc(d_weights, 16)
                        act.dma_start(w2g[:, :, :], W2.rearrange("(h p) d -> p h d", h=DH)).then_inc(d_weights, 16)
                        with nc.allow_non_contiguous_dma(reason="a few hundred words, once"):
                            act.dma_start(gn[:, 0, :], gnw.rearrange("(h p) -> p h", h=DH)).then_inc(d_weights, 16)
                            act.dma_start(gn[:, 1, :], gnb.rearrange("(h p) -> p h", h=DH)).then_inc(d_weights, 16)
                            for hf in range(DH):
                                act.dma_start(gateT[:, hf, :], gate[:, hf * P:(hf + 1) * P].rearrange("e p -> p e"))\
                                    .then_inc(d_weights, 16)
                    if experts:
                        load_weights(1, 0)
                        load_weights(1, 1)
                    for step in steps:
                        if step[0] == "attn":
                            attention(*step[1:])
                            if prepare and step[1:] == (0, 1):
                                act.wait_ge(s_v, 7)
                                for k in range(NA):
                                    j = min(k, AW)
                                    last = act.activation(aw[:, 0, k, :, :], aw32[:, k, :, :], ACT.Copy,
                                                          scale=ascale[:, j:j + 1])
                                last.then_inc(c_awhi, 1)
                        elif step[0] == "gather" and step[1] == 0:
                            hf = step[2]
                            act.wait_ge(m_g, hf + 1)
                            act.copy(taken(0, hf), turned[:, hf, :, :, 0:CAP]).then_inc(c_g, 1)
                        elif step[0] == "mm1":
                            e, f = step[1:]
                            m = FO * e + f
                            act.wait_ge(m_1, m + 1)
                            if m >= 4:
                                act.wait_ge(c_hl, m // 2 - 1)
                            act.activation(h1f[:, m // 2 % 2, m % 2, :], pf[:, m % 2, 0:SL], ACT.Gelu,
                                           scale=wsc[:, e, 0:1]).then_inc(c_gelu, 1)
                            if f == FO - 1 and e + 2 <= NE:
                                load_weights(e + 2, 0)
                            if f % 2 and f // 2 not in DVE_PAIRS:
                                act.wait_ge(c_gelu, m + 1)
                                if f == 1 and e >= 2:
                                    act.wait_ge(m_2, DH * (e - 1))
                                act.activation(h1[:, e % 2, 0, f - 1:f + 1, :], h1f[:, m // 2 % 2, :, :], ACT.Copy,
                                               scale=wsc[:, e, 1:2]).then_inc(c_hh, 1)
                        elif step[0] == "mm2" and step[2:] == (DH - 1, 1):
                            e = step[1]
                            if e:
                                act.wait_ge(m_b, e)
                            for dh in range(DH):
                                act.wait_ge(m_2, DH * e + dh + 1)
                                last = act.copy(yT[:, dh, :], pf[:, 2 + dh, 0:SL])
                            last.then_inc(c_yT, 1)
                            if e + 2 <= NE:
                                load_weights(e + 2, 1)
                        elif step[0] == "back":
                            e = step[1]
                            act.wait_ge(m_b, e + 1)
                            if e == 0:
                                act.wait_ge(c_slot, 2)
                            if e >= 2:
                                act.wait_ge(d_scat, 48 * (e - 1))
                            for c, (k0, n) in enumerate(SC):
                                bank, o = (2, D * c) if c < 2 else (3, 0)
                                act.activation(y[0:n, e % 2, c, :], pf[0:n, bank, o:o + D], ACT.Copy,
                                               scale=gs[0:n, e, c:c + 1]).then_inc(c_y, 1)
                        elif step[0] == "route":
                            act.wait_ge(c_soft, 2)
                            act.activation(lexp[:, :, :, :], ldif[:, :, :, :], ACT.Exp, scale=1.0 / XS)\
                                .then_inc(c_exp, 1)
                        elif step[0] == "hi" and step[2] == 0:
                            n = step[1]
                            e = (n + 1) % NE
                            act.wait_ge(p_sc, 4 * n + 4)
                            if n >= 2:
                                act.wait_ge(p_out[e % 2], 32 * (n // 2))
                            act.activation(wr[:, e % 2, 0, 0, :], raw[n % 2][:, 0, :], ACT.Copy, scale=wscale[:, 0:1])\
                                .then_inc(p_hi[0], 1)

                @block.vector
                def _(dve):
                    def normalise(src, stats, means, n, done, scale, out_, c_stats, c_means, c_scale):
                        for c in range(3):
                            last = dve.bn_stats(stats[:, c, :], src[:, c, :])
                        last.then_inc(c_stats, 1)
                        dve.wait_ge(c_stats, n)
                        for c in range(3):
                            last = dve.bn_aggr(means[:, c, :], stats[:, c, :])
                        last.then_inc(c_means, 1)
                        dve.wait_ge(c_means, n)
                        dve.wait_ge(c_scale, n)
                        for c in range(3):
                            last = dve.tensor_scalar(out_[:, c, :], src[:, c, :], means[:, c, 0:1], scale[:, c:c + 1],
                                                     ALU.subtract, ALU.mult)
                        last.then_inc(done, 1)

                    def scale_weights():
                        dve.wait_ge(d_weights, 16 * (7 + 3 * HPH))
                        dve.tensor_reduce(vsum[:, :], aw32[:, AV, :, :], AX.X, ALU.add).then_inc(s_v, 1)
                        dve.wait_ge(s_v, 1)
                        dve.tensor_scalar(vsum[:, :], vsum[:, :], -1.0 / HD, None, ALU.mult).then_inc(s_v, 1)
                        dve.wait_ge(s_v, 2)
                        for hf in range(DH):
                            last = dve.scalar_tensor_tensor(aw32[:, AV, hf, :], aw32[:, AV, hf, :], vsum[:, hf:hf + 1],
                                                            bd, ALU.add, ALU.mult)
                        last.then_inc(s_v, 1)
                        dve.wait_ge(s_v, 3)
                        dve.tensor_reduce(aam[:, 0:AW], aw32[:, 0:AW, :, :].rearrange("p k h n -> p k (h n)"), AX.X,
                                          ALU.max, apply_absolute_value=True)
                        dve.tensor_reduce(aam[:, AW:AW + 1], aw32[:, AW:NA, :, :].rearrange("p k h n -> p (k h n)"),
                                          AX.X, ALU.max, apply_absolute_value=True).then_inc(c_aam, 1)
                        dve.tensor_scalar(gn[:, :, :], gn[:, :, :], 2.0, None, ALU.mult)
                        dve.tensor_scalar(w2g[:, :, :], w2g[:, :, :], 0.5, None, ALU.mult)
                        dve.wait_ge(c_aamr, 1)
                        dve.tensor_scalar(aamr[:, :], aamr[:, :], 1e-18, None, ALU.max).then_inc(s_v, 1)
                        dve.wait_ge(s_v, 4)
                        dve.tensor_scalar(apw[:, :].bitcast(I32), aamr[:, :].bitcast(I32), 0x7F800000, None,
                                          ALU.bitwise_and).then_inc(s_v, 1)
                        dve.wait_ge(s_v, 5)
                        dve.reciprocal(apinv[:, :], apw[:, :])
                        dve.tensor_scalar(undo[:, 0:4], apw[:, :], 2.0 ** -14 / XS, None, ALU.mult)
                        dve.tensor_scalar(undo[:, 4:5], apw[:, AW:AW + 1], 2.0 ** -15 / XS, None, ALU.mult)\
                            .then_inc(s_v, 1)
                        dve.wait_ge(s_v, 6)
                        dve.tensor_scalar(ascale[:, :], apinv[:, :], 2.0 ** 14, None, ALU.mult).then_inc(s_v, 1)
                        dve.tensor_scalar(dq, dq, unq, None, ALU.mult)
                        dve.tensor_scalar(dk, dk, unk, None, ALU.mult)
                        dve.tensor_scalar(kd[0:HP, :, :], kd[0:HP, :, :], undo[0:HP, AK:AK + 1], None, ALU.mult)

                    def split_weights():
                        dve.wait_ge(s_v, 7)
                        dve.wait_ge(c_awhi, 1)
                        for k in range(NA):
                            j = min(k, AW)
                            last = dve.scalar_tensor_tensor(aw[:, 1, k, :, :], aw32[:, k, :, :], ascale[:, j:j + 1],
                                                            aw[:, 0, k, :, :], ALU.mult, ALU.subtract)
                        last.then_inc(c_ready, 1)

                    def score_mask(s, c, place):
                        n = CH[c][1]
                        src = pa[0:n, :, 256 * place:256 * (place + 1)].rearrange("p r (h n) -> p r h n", h=2)[:, :, :, 0:n]
                        dst = sc[0:n, c, :, 0:n].rearrange("p (h r) n -> p r h n", h=2)
                        m = mask[0:n, 0:n].unsqueeze(1).unsqueeze(1).broadcast_to([n, HPH, 2, n])
                        return dve.tensor_tensor(dst, src, m, ALU.mult)

                    def attention(s, p):
                        if p == 0:
                            dve.wait_ge(M_EMB, s + 1)
                            if s:
                                dve.wait_ge(d_h[s % 2], 16 * (s // 2 + s % 2))
                            dve.tensor_tensor(h[0:HP, s % 2, 0:2, :],
                                              p_emb[0:HP, b_emb, :].rearrange("p (c d) -> p c d", c=2), posb[0:HP, :, :],
                                              ALU.add).then_inc(c_h, 1)
                            dve.wait_ge(c_h, s + 1)
                            normalise(h[:, s % 2, :, :], st, mv, s + 1, c_xh, rs, xh_of(s), c_st, c_mv, c_rs)
                        elif p == 1:
                            dve.wait_ge(c_xThi, s + 1)
                            dve.scalar_tensor_tensor(xT[:, 1, :, :], pp[:, 1:3, 0:S], XS, xT[:, 0, :, :],
                                                     ALU.mult, ALU.subtract).then_inc(c_xT, 1)
                        elif p == 2:
                            dve.wait_ge(M_QK, s + 1)
                            dve.tensor_tensor(qT[:, :, :], pp[:, 0:2, 0:S], dq, ALU.mult).then_inc(c_q, 1)
                            dve.tensor_tensor(kT[:, :, :], pp[:, 2:4, 0:S], dk, ALU.mult).then_inc(c_k, 1)
                        elif p == 3:
                            dve.wait_ge(c_v, s + 1)
                            dve.tensor_tensor(
                                kt[0:HP, :, :].rearrange("p c (h e) -> p c h e", h=HEADS),
                                pp[0:HP, 0:2, D:2 * D].rearrange("p c (h e) -> p c h e", h=HEADS),
                                kd[0:HP, :, :].unsqueeze(3).broadcast_to([HP, 2, HEADS, HD]), ALU.mult)\
                                .then_inc(c_kt, 1)
                        elif p == 4:
                            dve.wait_ge(M_GS, s + 1)
                            dve.tensor_tensor(sbd[:, :, :, :].rearrange("p h u e -> p (h u) e"),
                                              pa[:, 0, :].rearrange("p (k e) -> p k e", k=4),
                                              bd.unsqueeze(1).broadcast_to([P, 4, P]), ALU.mult).then_inc(c_state, 1)
                            dve.wait_ge(c_state, 2 * s + 1)
                            dve.tensor_tensor(sbd[:, :, 1, :], sbd[:, :, 1, :], sbd[:, :, 0, :], ALU.add)\
                                .then_inc(c_state, 1)
                            dve.wait_ge(c_th, s + 1)
                            dve.scalar_tensor_tensor(s2[:, :, :], th[:, :, :], 1.0, pa[:, 2:4, 0:S], ALU.add, ALU.mult)\
                                .then_inc(c_s2, 1)
                        elif p == 5:
                            dve.wait_ge(M_SA, s + 1)
                            score_mask(s, 0, 0)
                            score_mask(s, 1, 1).then_inc(c_scA, 1)
                        elif p == 6:
                            dve.wait_ge(M_SB, s + 1)
                            score_mask(s, 2, 0).then_inc(c_scB, 1)
                        elif p == 7:
                            for k, (c0, c1, n) in enumerate(((0, 2, HP), (2, 3, NTXT))):
                                dve.wait_ge(c_sq, 2 * s + k + 1)
                                dve.tensor_reduce(ss[:, HEADS * c0:HEADS * c1],
                                                  sq[:, c0:c1, :].rearrange("p c (h e) -> p (c h) e", h=HEADS),
                                                  AX.X, ALU.add).then_inc(c_ss, 1)
                            for k, (c0, c1, n) in enumerate(((0, 2, HP), (2, 3, NTXT))):
                                dve.wait_ge(c_rg, 2 * s + k + 1)
                                dve.tensor_tensor(
                                    rn[0:n, c0:c1, :].rearrange("p c (h e) -> p c h e", h=HEADS),
                                    pa[0:n, k, 0:D * (c1 - c0)].rearrange("p (c h e) -> p c h e", h=HEADS, e=HD),
                                    rg[0:n, HEADS * c0:HEADS * c1].rearrange("p (c h) -> p c h", h=HEADS)
                                    .unsqueeze(3).broadcast_to([n, c1 - c0, HEADS, HD]), ALU.mult).then_inc(c_rn, 1)
                        elif p == 8:
                            dve.wait_ge(M_RT, s + 1)
                            dve.wait_ge(c_s2b, s + 1)
                            for hf in range(DH):
                                last = dve.scalar_tensor_tensor(oT[:, hf, :], pa[:, 2 + hf, 0:S], gn[:, 0, hf:hf + 1],
                                                                s2b[:, hf, :], ALU.mult, ALU.add)
                            last.then_inc(c_oT, 1)
                        elif p == 9:
                            dve.wait_ge(M_W2, s + 1)
                            if s >= 2:
                                dve.wait_ge(d_out[s % 2], 32 * (s // 2))
                            dve.tensor_tensor(h2[0:HP, s % 2, 0:2, :],
                                              pa[0:HP, 0, :].rearrange("p (c d) -> p c d", c=2),
                                              h[0:HP, s % 2, 0:2, :], ALU.add)
                            dve.tensor_tensor(h2[:, s % 2, 2, :], pa[:, 1, 0:D], h[:, s % 2, 2, :], ALU.add)\
                                .then_inc(c_h2, 1)
                            dve.wait_ge(c_h2, s + 1)
                            if s:
                                dve.wait_ge(c_hi, s)
                                dve.wait_ge(c_lo, s)
                            normalise(h2[:, s % 2, :, :], st2, mv2, s + 1, c_xs, rs2x, xs, c_st2, c_mv2, c_rs2x)
                        elif p == 11:
                            dve.wait_ge(M_RTR, s + 1)
                            dve.tensor_copy(lg[:, :, :, s], pa[:, 3, 0:3 * NE].rearrange("p (c e) -> p c e", c=3))\
                                .then_inc(c_lg, 1)

                    def softmax():
                        dve.wait_ge(c_lg, G)
                        over = lg[:, :, :, :].rearrange("p c e s -> p c s e")
                        dve.tensor_reduce(lmax[:, :, :], over, AX.X, ALU.max).then_inc(c_soft, 1)
                        dve.wait_ge(c_soft, 1)
                        dve.tensor_tensor(ldif[:, :, :, :], lg[:, :, :, :],
                                          lmax[:, :, :].unsqueeze(2).broadcast_to([P, 3, NE, G]), ALU.subtract)\
                            .then_inc(c_soft, 1)
                        dve.wait_ge(c_exp, 1)
                        dve.tensor_reduce(lsum[:, :, :], lexp[:, :, :, :].rearrange("p c e s -> p c s e"), AX.X, ALU.add)\
                            .then_inc(c_soft, 1)
                        dve.wait_ge(c_soft, 3)
                        dve.reciprocal(lrec[:, :, :], lsum[:, :, :]).then_inc(c_soft, 1)
                        dve.wait_ge(c_soft, 4)
                        dve.tensor_tensor(prob[:, :, :, :], lexp[:, :, :, :],
                                          lrec[:, :, :].unsqueeze(2).broadcast_to([P, 3, NE, G]), ALU.mult)\
                            .then_inc(c_prob, 1)

                    def choose(r):
                        if r < 0:
                            dve.wait_ge(m_pT, 1)
                            dve.tensor_copy(val[:, 0, 0:S], pa[0:ROWS, 1, 0:S]).then_inc(c_val, 1)
                            dve.wait_ge(c_val, 1)
                        else:
                            k = slice(8 * r, 8 * r + 8)
                            src, dst = val[:, 0 if r == 0 else 1, :], val[:, 1, :]
                            dve.max(top[:, k], src).then_inc(c_top, 1)
                            dve.wait_ge(c_top, 3 * r + 1)
                            dve.max_index(topi[:, k], top[:, k], src).then_inc(c_top, 1)
                            dve.match_replace(dst, top[:, k], src, -1.0).then_inc(c_top, 1)
                            dve.wait_ge(c_top, 3 * r + 3)

                    def chosen():
                        if experts:
                            dve.wait_ge(d_c2, 16)
                        dve.tensor_copy(pack[:, :, 1], top[:, NSENT:])
                        dve.tensor_scalar(pack[:, :, 0], topi[:, NSENT:], rowbase, None, ALU.add).then_inc(c_pick, 1)

                    def slots():
                        dve.wait_ge(d_tail, 16 * 3)
                        dve.tensor_scalar(slout[:, :, :], slot[:, :, :, 0], base[:, 0:1], None, ALU.add)\
                            .then_inc(c_slot, 1)
                        dve.tensor_tensor(gs[:, :, :], slot[:, :, :, 1],
                                          wsc[:, :, 2:3].broadcast_to([P, NE, 3]), ALU.mult).then_inc(c_slot, 1)
                        dve.wait_ge(c_slot, 1)
                        dve.tensor_scalar(base[:, :], base[:, :], float(G * S), None, ALU.add)

                    def gathered(e, hf):
                        dve.wait_ge(m_g, DH * e + hf + 1)
                        dve.tensor_copy(taken(e, hf), turned[:, hf, :, :, 0:CAP]).then_inc(c_g, 1)

                    def split(e, f):
                        q, k = (FO * e + f) // 2, f // 2
                        hi, pair = h1[:, e % 2, 0, f - 1:f + 1, :], h1f[:, q % 2, :, :]
                        if k in DVE_PAIRS:
                            dve.wait_ge(c_gelu, 2 * q + 2)
                            dve.tensor_scalar(hi, pair, wsc[:, e, 1:2], None, ALU.mult).then_inc(c_hd, 1)
                            dve.wait_ge(c_hd, len(DVE_PAIRS) * e + DVE_PAIRS.index(k) + 1)
                        else:
                            dve.wait_ge(c_hh, ACT_PAIRS * e + k - sum(j < k for j in DVE_PAIRS) + 1)
                        dve.scalar_tensor_tensor(h1[:, e % 2, 1, f - 1:f + 1, :], pair, wsc[:, e, 1:2], hi,
                                                 ALU.mult, ALU.subtract).then_inc(c_hl, 1)

                    def prepare_reduce(n, k):
                        if n:
                            dve.wait_ge(p_amr, n)
                        dve.wait_ge(d_raw[n % 2], 32 * (n // 2 + 1))
                        last = dve.tensor_reduce(am[:, k:k + 1], raw[n % 2][:, k, :], AX.X, ALU.max,
                                                 apply_absolute_value=True)
                        if k:
                            last.then_inc(p_am, 1)

                    def prepare_scales(n):
                        e = (n + 1) % NE
                        dve.wait_ge(p_amr, n + 1)
                        if n:
                            for k in range(2):
                                dve.wait_ge(p_hi[k], n)
                        dve.tensor_scalar(amc[:, :], amr[:, :], 1e-18, None, ALU.max).then_inc(p_sc, 1)
                        dve.wait_ge(p_sc, 4 * n + 1)
                        dve.tensor_scalar(pw[:, :].bitcast(I32), amc[:, :].bitcast(I32), 0x7F800000, None,
                                          ALU.bitwise_and).then_inc(p_sc, 1)
                        dve.wait_ge(p_sc, 4 * n + 2)
                        dve.reciprocal(pinv[:, :], pw[:, :]).then_inc(p_sc, 1)
                        dve.wait_ge(p_sc, 4 * n + 3)
                        dve.tensor_scalar(wscale[:, :], pinv[:, :], 2.0 ** 14, None, ALU.mult)
                        dve.tensor_scalar(wsc[:, e, 0:1], pw[:, 0:1], 2.0 ** -14 / XS, None, ALU.mult)
                        dve.tensor_scalar(wsc[:, e, 1:2], pinv[:, 0:1], 2.0 ** 6, None, ALU.mult)
                        dve.scalar_tensor_tensor(wsc[:, e, 2:3], pw[:, 0:1], 2.0 ** -20, pw[:, 1:2], ALU.mult, ALU.mult)\
                            .then_inc(p_sc, 1)

                    def prepare_lo(n, k):
                        e = (n + 1) % NE
                        dve.wait_ge(p_sc, 4 * n + 4)
                        dve.wait_ge(p_hi[k], n + 1)
                        dve.scalar_tensor_tensor(wr[:, e % 2, k, 1, :], raw[n % 2][:, k, :], wscale[:, k:k + 1],
                                                 wr[:, e % 2, k, 0, :], ALU.mult, ALU.subtract).then_inc(p_lo, 1)

                    for step in steps:
                        if step[0] == "attn":
                            attention(*step[1:])
                            if prepare and step[1:] == (0, 0):
                                scale_weights()
                            if prepare and step[1:] == (0, 1):
                                split_weights()
                        elif step[0] == "gather" and step[1]:
                            gathered(*step[1:])
                        elif step[0] == "mm1" and step[2] % 2:
                            split(*step[1:])
                        elif step[0] == "route":
                            softmax()
                        elif step[0] == "choose":
                            choose(step[1])
                        elif step[0] == "topk":
                            chosen()
                        elif step == ("mm2", 0, 0, 0):
                            slots()
                        elif step[0] == "reduce":
                            prepare_reduce(*step[1:])
                        elif step[0] == "scales":
                            prepare_scales(step[1])
                        elif step[0] == "lo":
                            prepare_lo(*step[1:])

                    if attend:
                        if experts:
                            for k in range(2):
                                dve.wait_ge(d_gath[k], 16 * G * (NE // 2))
                        dve.wait_ge(m_iT, 1)
                        dve.tensor_copy(idx[:, :], pa[0:CAP, 0, 0:ROWS])

                @block.gpsimd
                def _(pool):
                    def power(src, n, c_in, mid, c_mid, dst, c_out, width, mul):
                        pool.wait_ge(c_in, n)
                        pool.tensor_scalar(mid, src, mul, EPS, ALU.mult, ALU.add).then_inc(c_mid, 1)
                        pool.wait_ge(c_mid, n)
                        return pool.tensor_tensor(dst, mid, nhalf[:, 0:width], ALU.pow).then_inc(c_out, 1)

                    def attention(s, p):
                        if p == 0:
                            power(mv[:, :, 1], s + 1, c_mv, ve[:, :], c_ve, rs[:, :], c_rs, 3, 1.0)
                        elif p == 4:
                            pool.wait_ge(c_s2, s + 1)
                            if prepare and s == 0:
                                pool.wait_ge(c_ready, 1)
                            for hf in range(DH):
                                last = pool.tensor_scalar(s2b[:, hf, :], s2[:, hf, :], unw, gn[:, 1, hf:hf + 1],
                                                          ALU.mult, ALU.add)
                            last.then_inc(c_s2b, 1)
                        elif p == 7:
                            for k, (a, b) in enumerate(((0, 2 * HEADS), (2 * HEADS, 3 * HEADS))):
                                power(ss[:, a:b], 2 * s + k + 1, c_ss, ssb[:, a:b], c_ssb, rg[:, a:b], c_rg,
                                      b - a, 1.0 / HD)
                        elif p == 9:
                            power(mv2[:, :, 1], s + 1, c_mv2, ve2[:, :], c_ve2, rs2[:, :], c_rs2, 3, 1.0)
                            pool.wait_ge(c_rs2, s + 1)
                            pool.tensor_scalar(rs2x[:, :], rs2[:, :], XS, 0.0, ALU.mult, ALU.add).then_inc(c_rs2x, 1)
                        elif p == 10:
                            pool.wait_ge(c_hi, s + 1)
                            pool.tensor_tensor(xhl[:, s % 2, :, 1, :], xs[:, :, :], xhl[:, s % 2, :, 0, :], ALU.subtract)\
                                .then_inc(c_lo, 1)

                    def fetch(e):
                        if e >= 2:
                            pool.wait_ge(m_g, DH * (e - 1))
                        for s in range(G):
                            k = G * e + s
                            pool.indirect_dma_start(
                                out=xg[0:CAP, e % 2, s, :], out_offset=None, in_=scr_x[1 - parity],
                                in_offset=bass.IndirectOffsetOnAxis(ap=idx[:, k:k + 1], axis=0))\
                                .then_inc(d_gath[e % 2], 16)

                    if experts:
                        fetch(0)
                        fetch(1)
                    for step in steps:
                        if step[0] == "attn":
                            attention(*step[1:])
                            if prepare and step[1:] == (0, 0):
                                pool.wait_ge(c_aam, 1)
                                pool.partition_all_reduce(aamr[:, :], aam[:, :], P, RADD_MAX).then_inc(c_aamr, 1)
                        elif step[0] == "gather" and step[2] == DH - 1 and step[1] + 2 < NE:
                            fetch(step[1] + 2)
                        elif step[0] == "back":
                            e = step[1]
                            if e == 0:
                                pool.wait_ge(c_slot, 1)
                            pool.wait_ge(c_y, 3 * e + 3)
                            if e:
                                pool.wait_ge(d_scat, 48 * e)
                            for c, (k0, n) in enumerate(SC):
                                pool.indirect_dma_start(
                                    out=out_rows, out_offset=bass.IndirectOffsetOnAxis(ap=slout[0:n, e, c:c + 1], axis=0),
                                    in_=y[0:n, e % 2, c, :], in_offset=None, compute_op=ALU.add).then_inc(d_scat, 16)
                        elif step[0] == "hi" and step[2] == 1:
                            n = step[1]
                            e = (n + 1) % NE
                            pool.wait_ge(p_sc, 4 * n + 4)
                            if n >= 2:
                                pool.wait_ge(p_out[e % 2], 32 * (n // 2))
                            pool.tensor_scalar(wr[:, e % 2, 1, 0, :], raw[n % 2][:, 1, :], wscale[:, 1:2], None,
                                               ALU.mult).then_inc(p_hi[1], 1)
                        elif step[0] == "reduce" and step[2] == 1:
                            n = step[1]
                            pool.wait_ge(p_am, n + 1)
                            if n:
                                pool.wait_ge(p_sc, 4 * n)
                            pool.partition_all_reduce(amr[:, :], am[:, :], P, RADD_MAX).then_inc(p_amr, 1)
                    if attend:
                        pool.wait_ge(c_lo, G)
                    if experts:
                        pool.wait_ge(d_scat, 48 * NE)
                        for k in range(2):
                            pool.wait_ge(d_gath[k], 16 * G * (NE // 2))
                        pool.dma_reset(range(d_scat.num, d_gath[1].num + 1))
            barrier()

        body(0, 0, True, False, prepare=True)
        with nc.Fori(0, (NG - 2) // 2) as k:
            body(2 * k + 1, 1, True, True)
            body(2 * k + 2, 0, True, True)
        body(NG - 1, 1, True, True, ahead=False)
        body(NG, 0, False, True, more=False)


def constants():
    import numpy as np

    gamma = (1.0 - np.exp(np.linspace(np.log(1.0 / 512.0), np.log(1.0 / 32.0), HEADS))).astype(np.float32)
    gamma = gamma.astype(np.float64)
    t = np.zeros((P, C_ALL), np.float32)
    n, p = np.arange(S), np.arange(P)
    for hf in range(DH):
        per_row = gamma[HPH * hf + p // HD]
        t[:, C_DQ + S * hf:C_DQ + S * (hf + 1)] = per_row[:, None] ** n
        t[:, C_DK + S * hf:C_DK + S * (hf + 1)] = per_row[:, None] ** -n.astype(np.float64)
    for c in range(2):
        t[0:HP, C_KD + HEADS * c:C_KD + HEADS * (c + 1)] = gamma[None] ** -(HP * c + np.arange(HP, dtype=np.float64))[:, None]
    t[:, C_MASK:C_BD] = p[None] >= p[:, None]
    t[:, C_BD:C_ID] = p[None] // HD == p[:, None] // HD
    t[:, C_ID:C_ROW] = np.eye(P)
    t[0:ROWS, C_ROW] = S * (np.arange(ROWS) % G)
    return t


_INS = ["x", "txt", "L0_tok_W_embed", "L0_tok_b_embed", "L0_tok_pos_embed", "L0_attn_Wq", "L0_attn_Wk",
        "L0_attn_Wv", "L0_attn_W1", "L0_attn_W2", "L0_attn_gn_w", "L0_attn_gn_b", "L0_ffn_gate_w",
        "L0_ffn_w1", "L0_ffn_w2"]


def kernel(**inputs):
    import numpy as _np
    import concourse.bacc as _bacc
    from concourse import mybir as _mybir
    from concourse.bass_utils import run_bass_kernel_spmd as _run

    nc = _bacc.Bacc("TRN2", target_bir_lowering=False, num_devices=1)
    arrays, args = {}, []
    for name, a in [(n, inputs[n]) for n in _INS] + [("constants", constants())]:
        a = _np.ascontiguousarray(a)
        arrays[f"in_{name}_dram"] = a
        args.append(nc.dram_tensor(f"in_{name}_dram", a.shape, _mybir.dt.from_np(a.dtype), kind="ExternalInput").ap())
    args.append(nc.dram_tensor("out_dram", (B, S, D), F32, kind="ExternalOutput").ap())
    build(nc, *args)
    r = _run(nc, [arrays], core_ids=[0])
    return r.results[0]["out_dram"]
```
